# Optimizing a Trainium2 kernel written in Bass

```python
import numpy as np
import jax
import jax.numpy as jnp

def _softmax(x, axis=-1):
    return jax.nn.softmax(x, axis=axis)

def _gelu(x):
    return jax.nn.gelu(x, approximate=True)

def _silu(x):
    return jax.nn.silu(x)

def _sigmoid(x):
    return jax.nn.sigmoid(x)

def _layernorm(x, axis=-1, eps=1e-05):
    m = jnp.mean(x, axis=axis, keepdims=True)
    v = jnp.var(x, axis=axis, keepdims=True)
    return (x - m) / jnp.sqrt(v + eps)

def _scatter_add(tgt, idx, src, axis=0):
    return tgt.at[idx].add(src)

def _segment_sum(src, seg, n):
    return jax.ops.segment_sum(src, seg, n)
kernel_name = 'mk_adaln_attn_ffn_d1_seqx_r8_9f5fc6'

def setup_inputs(seed: int=0):
    np.random.seed(seed)
    _w = jnp.asarray

    def _rec_inputs():
        import jax
        import jax.numpy as jnp
        _rk = jax.random.key(seed)
        x = 7.22e-05 + 1 * jax.random.normal(jax.random.fold_in(_rk, 1), (8, 128, 128), jnp.float32)
        _lenS = 128 - jax.random.randint(jax.random.fold_in(_rk, 7), (8,), 0, max(1, 128 // 4) + 1, jnp.int32)
        _lenS2 = 128 - jax.random.randint(jax.random.fold_in(_rk, 8), (8,), 0, max(1, 128 // 4) + 1, jnp.int32)
        itok_B_0_2 = jax.random.randint(jax.random.fold_in(_rk, 11), (8,), 0, 3, jnp.int32)
        itok_B_0_8 = jax.random.randint(jax.random.fold_in(_rk, 12), (8,), 0, 9, jnp.int32)
        return (x, itok_B_0_2, itok_B_0_8)
    x, itok_B_0_2, itok_B_0_8 = _rec_inputs()

    def _L0_cond_setup():
        import jax, jax.numpy as jnp
        import numpy as np
        B, S, D, F, E = (8, 128, 128, 512, 4)

        def _dense(x, wi, wo):
            return jax.nn.relu(x @ wi) @ wo
        key = jax.random.key(seed)
        ks = jax.random.split(key, 10)
        scale = 0.02
        return {'hidden_states': jax.random.normal(ks[0], (B, S, D), jnp.float32), 'type_idx': jax.random.randint(ks[1], (B,), 0, 3, jnp.int32), 'expert_wi': jax.random.normal(ks[2], (E, D, F), jnp.float32) * scale, 'expert_wo': jax.random.normal(ks[3], (E, F, D), jnp.float32) * scale, 'share_wi': jax.random.normal(ks[4], (3, D, F), jnp.float32) * scale, 'share_wo': jax.random.normal(ks[5], (3, F, D), jnp.float32) * scale, 'gate_vecs': jnp.array([[0.22, 0.22, 0.2, 0.2], [0.2, 0.22, 0.22, 0.2], [0.2, 0.2, 0.22, 0.22]], jnp.float32), 'gate_w1': jax.random.normal(ks[6], (4 * D, D), jnp.float32) * scale, 'gate_w2': jax.random.normal(ks[7], (D, 4), jnp.float32) * scale}
    _L0_cond_all = _L0_cond_setup()
    _L0_cond_in = {k: v for k, v in _L0_cond_all.items() if k in ('expert_wi', 'expert_wo', 'share_wi', 'share_wo', 'gate_vecs', 'gate_w1', 'gate_w2')}
    del _L0_cond_all

    def _L0_attn_setup():
        import jax, jax.numpy as jnp
        import numpy as np
        B, S, D = (2, 256, 128)
        H, DH = (16, 64)
        SCALE = DH ** (-0.5)
        key = jax.random.key(seed)
        ks = jax.random.split(key, 5)

        def w(k, shape):
            return jax.random.normal(k, shape, dtype=jnp.float32) * 0.02
        return {'x': jax.random.normal(ks[0], (B, S, D), dtype=jnp.float32), 'Wq': w(ks[1], (D, H * DH)), 'Wk': w(ks[2], (D, H * DH)), 'Wv': w(ks[3], (D, H * DH)), 'Wo': w(ks[4], (H * DH, D)), 'bo': jnp.zeros((D,), dtype=jnp.float32)}
    _L0_attn_all = _L0_attn_setup()
    _L0_attn_in = {k: v for k, v in _L0_attn_all.items() if k in ('Wq', 'Wk', 'Wv', 'Wo', 'bo')}
    del _L0_attn_all

    def _L0_cond2_setup():
        import jax, jax.numpy as jnp
        import numpy as np
        LN_EPS = 1e-05
        key = jax.random.key(seed)
        ks = jax.random.split(key, 8)
        B, S, H, A, L = (32, 256, 128, 32, 10)
        return {'hidden_states': jax.random.normal(ks[0], (B, S, H), dtype=jnp.float32), 'language_ids': jax.random.randint(ks[1], (B,), 0, L, dtype=jnp.int64), 'W1': jax.random.normal(ks[2], (L, H, A), dtype=jnp.float32) * (1.0 / np.sqrt(H)), 'b1': jnp.zeros((L, A), dtype=jnp.float32), 'W2': jax.random.normal(ks[3], (L, A, H), dtype=jnp.float32) * (1.0 / np.sqrt(A)), 'b2': jnp.zeros((L, H), dtype=jnp.float32), 'gamma': jnp.ones((L, H), dtype=jnp.float32), 'beta': jnp.zeros((L, H), dtype=jnp.float32)}
    _L0_cond2_all = _L0_cond2_setup()
    _L0_cond2_in = {k: v for k, v in _L0_cond2_all.items() if k in ('W1', 'b1', 'W2', 'b2', 'gamma', 'beta')}
    del _L0_cond2_all

    def _L0_ffn_setup():
        import jax, jax.numpy as jnp
        import numpy as np
        B, T, C, H, E, K, F = (2, 256, 128, 16, 8, 2, 256)
        EPS = 1e-05

        def layernorm(x, w):
            m = x.mean(-1, keepdims=True)
            v = x.var(-1, keepdims=True)
            return (x - m) * jax.lax.rsqrt(v + EPS) * w

        def attention(x, c_attn_w, c_proj_w):
            b, t, c = x.shape
            hd = c // H
            q, k, v = jnp.split(x @ c_attn_w, 3, axis=-1)
            q = q.reshape(b, t, H, hd).transpose(0, 2, 1, 3)
            k = k.reshape(b, t, H, hd).transpose(0, 2, 1, 3)
            v = v.reshape(b, t, H, hd).transpose(0, 2, 1, 3)
            att = jnp.einsum('bhqd,bhkd->bhqk', q, k) / jnp.sqrt(jnp.asarray(hd, x.dtype))
            causal = jnp.tril(jnp.ones((t, t), bool))
            att = jnp.where(causal, att, jnp.asarray(-jnp.inf, att.dtype))
            att = jax.nn.softmax(att, axis=-1)
            y = jnp.einsum('bhqk,bhkd->bhqd', att, v)
            y = y.transpose(0, 2, 1, 3).reshape(b, t, c)
            return y @ c_proj_w

        def moe_mlp(x, router_w, w1, w2):
            b, t, c = x.shape
            xf = x.reshape(-1, c)
            router_logits = xf @ router_w
            probs = jax.nn.softmax(router_logits.astype(jnp.float32), axis=-1)
            rw, sel = jax.lax.top_k(probs, K)
            rw = rw / rw.sum(axis=-1, keepdims=True)
            rw = rw.astype(x.dtype)
            w1e = w1.reshape(c, E, F).transpose(1, 0, 2)
            w2e = w2.reshape(E, F, c)
            h = jax.nn.gelu(jnp.einsum('nc,ecf->enf', xf, w1e), approximate=False)
            y_all = jnp.einsum('enf,efc->nec', h, w2e)
            y_sel = jnp.take_along_axis(y_all, sel[:, :, None], axis=1)
            y = (y_sel * rw[:, :, None]).sum(axis=1)
            return y.reshape(b, t, c)
        key = jax.random.key(seed)
        ks = jax.random.split(key, 6)
        s = 0.02
        return {'x': jax.random.normal(ks[0], (B, T, C), jnp.float32), 'ln1_w': jnp.ones((C,), jnp.float32), 'c_attn_w': jax.random.normal(ks[1], (C, 3 * C), jnp.float32) * s, 'c_proj_w': jax.random.normal(ks[2], (C, C), jnp.float32) * s, 'ln2_w': jnp.ones((C,), jnp.float32), 'router_w': jax.random.normal(ks[3], (C, E), jnp.float32) * s, 'w1': jnp.clip(jax.random.normal(ks[4], (C, E * F), jnp.float32) * s, -0.06, 0.06), 'w2': jnp.clip(jax.random.normal(ks[5], (E * F, C), jnp.float32) * s, -0.06, 0.06)}
    _L0_ffn_all = _L0_ffn_setup()
    _L0_ffn_in = {k: v for k, v in _L0_ffn_all.items() if k in ('ln1_w', 'c_attn_w', 'c_proj_w', 'ln2_w', 'router_w', 'w1', 'w2')}
    del _L0_ffn_all
    return {'x': x, 'itok_B_0_2': itok_B_0_2, 'itok_B_0_8': itok_B_0_8, 'L0_cond_expert_wi': _L0_cond_in['expert_wi'], 'L0_cond_expert_wo': _L0_cond_in['expert_wo'], 'L0_cond_share_wi': _L0_cond_in['share_wi'], 'L0_cond_share_wo': _L0_cond_in['share_wo'], 'L0_cond_gate_vecs': _L0_cond_in['gate_vecs'], 'L0_cond_gate_w1': _L0_cond_in['gate_w1'], 'L0_cond_gate_w2': _L0_cond_in['gate_w2'], 'L0_attn_Wq': _L0_attn_in['Wq'], 'L0_attn_Wk': _L0_attn_in['Wk'], 'L0_attn_Wv': _L0_attn_in['Wv'], 'L0_attn_Wo': _L0_attn_in['Wo'], 'L0_attn_bo': _L0_attn_in['bo'], 'L0_cond2_W1': _L0_cond2_in['W1'], 'L0_cond2_b1': _L0_cond2_in['b1'], 'L0_cond2_W2': _L0_cond2_in['W2'], 'L0_cond2_b2': _L0_cond2_in['b2'], 'L0_cond2_gamma': _L0_cond2_in['gamma'], 'L0_cond2_beta': _L0_cond2_in['beta'], 'L0_ffn_ln1_w': _L0_ffn_in['ln1_w'], 'L0_ffn_c_attn_w': _L0_ffn_in['c_attn_w'], 'L0_ffn_c_proj_w': _L0_ffn_in['c_proj_w'], 'L0_ffn_ln2_w': _L0_ffn_in['ln2_w'], 'L0_ffn_router_w': _L0_ffn_in['router_w'], 'L0_ffn_w1': _L0_ffn_in['w1'], 'L0_ffn_w2': _L0_ffn_in['w2']}

def reference(x, itok_B_0_2, itok_B_0_8, L0_cond_expert_wi, L0_cond_expert_wo, L0_cond_share_wi, L0_cond_share_wo, L0_cond_gate_vecs, L0_cond_gate_w1, L0_cond_gate_w2, L0_attn_Wq, L0_attn_Wk, L0_attn_Wv, L0_attn_Wo, L0_attn_bo, L0_cond2_W1, L0_cond2_b1, L0_cond2_W2, L0_cond2_b2, L0_cond2_gamma, L0_cond2_beta, L0_ffn_ln1_w, L0_ffn_c_attn_w, L0_ffn_c_proj_w, L0_ffn_ln2_w, L0_ffn_router_w, L0_ffn_w1, L0_ffn_w2):
    import jax
    import jax.numpy as jnp

    def _L0_cond_ref(hidden_states, type_idx, expert_wi, expert_wo, share_wi, share_wo, gate_vecs, gate_w1, gate_w2):
        import jax, jax.numpy as jnp
        import numpy as np
        B, S, D, F, E = (8, 128, 128, 512, 4)

        def _dense(x, wi, wo):
            return jax.nn.relu(x @ wi) @ wo
        s0 = _dense(hidden_states, share_wi[0], share_wo[0])
        s1 = _dense(hidden_states, share_wi[1], share_wo[1])
        s2 = _dense(hidden_states, share_wi[2], share_wo[2])
        idx_a = type_idx
        idx_b = type_idx + 1
        out_a = jnp.einsum('bsf,bfd->bsd', jax.nn.relu(jnp.einsum('bsd,bdf->bsf', hidden_states, expert_wi[idx_a])), expert_wo[idx_a])
        out_b = jnp.einsum('bsf,bfd->bsd', jax.nn.relu(jnp.einsum('bsd,bdf->bsf', hidden_states, expert_wi[idx_b])), expert_wo[idx_b])
        p = jax.nn.softmax(gate_vecs / 0.1, axis=-1)
        wa = p[type_idx, idx_a][:, None, None]
        wb = p[type_idx, idx_b][:, None, None]
        expert_out = out_a * wa + out_b * wb
        gi = jnp.concatenate([expert_out[:, 0], s0[:, 0], s1[:, 0], s2[:, 0]], axis=-1)
        g = jax.nn.softmax(jax.nn.relu(gi @ gate_w1) @ gate_w2, axis=-1)
        out = expert_out * g[:, 0, None, None] + s0 * g[:, 1, None, None] + s1 * g[:, 2, None, None] + s2 * g[:, 3, None, None]
        return out

    def _L0_attn_ref(x, Wq, Wk, Wv, Wo, bo):
        import jax, jax.numpy as jnp
        import numpy as np
        B, S, D = (2, 256, 128)
        H, DH = (16, 64)
        SCALE = DH ** (-0.5)
        b, s, _ = x.shape
        q = (x @ Wq).reshape(b, s, H, DH)
        k = (x @ Wk).reshape(b, s, H, DH)
        v = (x @ Wv).reshape(b, s, H, DH)
        scores = jnp.einsum('bqhd,bkhd->bhqk', q, k) * SCALE
        attn = jax.nn.softmax(scores, axis=-1)
        out = jnp.einsum('bhqk,bkhd->bqhd', attn, v).reshape(b, s, H * DH)
        return out @ Wo + bo

    def _L0_cond2_ref(hidden_states, language_ids, W1, b1, W2, b2, gamma, beta):
        import jax, jax.numpy as jnp
        import numpy as np
        LN_EPS = 1e-05
        w1 = W1[language_ids]
        w2 = W2[language_ids]
        h = jnp.einsum('bsh,bha->bsa', hidden_states, w1) + b1[language_ids][:, None, :]
        h = jax.nn.relu(h)
        adapted = jnp.einsum('bsa,bah->bsh', h, w2) + b2[language_ids][:, None, :]
        x = hidden_states + adapted
        mean = jnp.mean(x, axis=-1, keepdims=True)
        var = jnp.mean(jnp.square(x - mean), axis=-1, keepdims=True)
        normed = (x - mean) * jax.lax.rsqrt(var + LN_EPS)
        return normed * gamma[language_ids][:, None, :] + beta[language_ids][:, None, :]

    def _L0_ffn_ref(x, ln1_w, c_attn_w, c_proj_w, ln2_w, router_w, w1, w2):
        import jax, jax.numpy as jnp
        import numpy as np
        B, T, C, H, E, K, F = (2, 256, 128, 16, 8, 2, 256)
        EPS = 1e-05

        def layernorm(x, w):
            m = x.mean(-1, keepdims=True)
            v = x.var(-1, keepdims=True)
            return (x - m) * jax.lax.rsqrt(v + EPS) * w

        def attention(x, c_attn_w, c_proj_w):
            b, t, c = x.shape
            hd = c // H
            q, k, v = jnp.split(x @ c_attn_w, 3, axis=-1)
            q = q.reshape(b, t, H, hd).transpose(0, 2, 1, 3)
            k = k.reshape(b, t, H, hd).transpose(0, 2, 1, 3)
            v = v.reshape(b, t, H, hd).transpose(0, 2, 1, 3)
            att = jnp.einsum('bhqd,bhkd->bhqk', q, k) / jnp.sqrt(jnp.asarray(hd, x.dtype))
            causal = jnp.tril(jnp.ones((t, t), bool))
            att = jnp.where(causal, att, jnp.asarray(-jnp.inf, att.dtype))
            att = jax.nn.softmax(att, axis=-1)
            y = jnp.einsum('bhqk,bhkd->bhqd', att, v)
            y = y.transpose(0, 2, 1, 3).reshape(b, t, c)
            return y @ c_proj_w

        def moe_mlp(x, router_w, w1, w2):
            b, t, c = x.shape
            xf = x.reshape(-1, c)
            router_logits = xf @ router_w
            probs = jax.nn.softmax(router_logits.astype(jnp.float32), axis=-1)
            rw, sel = jax.lax.top_k(probs, K)
            rw = rw / rw.sum(axis=-1, keepdims=True)
            rw = rw.astype(x.dtype)
            w1e = w1.reshape(c, E, F).transpose(1, 0, 2)
            w2e = w2.reshape(E, F, c)
            h = jax.nn.gelu(jnp.einsum('nc,ecf->enf', xf, w1e), approximate=False)
            y_all = jnp.einsum('enf,efc->nec', h, w2e)
            y_sel = jnp.take_along_axis(y_all, sel[:, :, None], axis=1)
            y = (y_sel * rw[:, :, None]).sum(axis=1)
            return y.reshape(b, t, c)
        x = x + attention(layernorm(x, ln1_w), c_attn_w, c_proj_w)
        x = x + moe_mlp(layernorm(x, ln2_w), router_w, w1, w2)
        return x
    x = x + _L0_attn_ref(_L0_cond_ref(x, itok_B_0_2, L0_cond_expert_wi, L0_cond_expert_wo, L0_cond_share_wi, L0_cond_share_wo, L0_cond_gate_vecs, L0_cond_gate_w1, L0_cond_gate_w2), L0_attn_Wq, L0_attn_Wk, L0_attn_Wv, L0_attn_Wo, L0_attn_bo)
    x = x + _L0_ffn_ref(_L0_cond2_ref(x, itok_B_0_8, L0_cond2_W1, L0_cond2_b1, L0_cond2_W2, L0_cond2_b2, L0_cond2_gamma, L0_cond2_beta), L0_ffn_ln1_w, L0_ffn_c_attn_w, L0_ffn_c_proj_w, L0_ffn_ln2_w, L0_ffn_router_w, L0_ffn_w1, L0_ffn_w2)
    return x

_drawn_inputs = setup_inputs


def setup_inputs(seed=0):
    import zlib

    import numpy as np

    out = dict(_drawn_inputs(seed))
    spreads = {'L0_attn_bo': (0.0, 2.0),
     'L0_cond2_b1': (0.0, 2.0),
     'L0_cond2_b2': (0.0, 2.0),
     'L0_cond2_gamma': (1.0, 0.6),
     'L0_cond2_beta': (0.0, 0.8),
     'L0_ffn_ln1_w': (1.0, 0.6),
     'L0_ffn_ln2_w': (1.0, 0.6)}
    factors = {'L0_cond_expert_wi': 8.0,
     'L0_cond_expert_wo': 8.0,
     'L0_cond_share_wi': 8.0,
     'L0_cond_share_wo': 8.0,
     'L0_cond_gate_vecs': 8.0,
     'L0_cond_gate_w1': 8.0,
     'L0_cond_gate_w2': 8.0,
     'L0_attn_Wq': 8.0,
     'L0_attn_Wk': 8.0,
     'L0_attn_Wv': 8.0,
     'L0_attn_Wo': 8.0,
     'L0_ffn_c_attn_w': 4.845,
     'L0_ffn_c_proj_w': 4.969,
     'L0_ffn_router_w': 4.529,
     'L0_ffn_w1': 3.96,
     'L0_ffn_w2': 3.881}
    for name, (base, spread) in spreads.items():
        noise = np.random.default_rng([zlib.crc32(name.encode()), seed]).standard_normal(out[name].shape)
        drawn = base * np.exp(spread * noise) if base else spread * noise
        out[name] = jnp.asarray(drawn.astype(out[name].dtype))
    for name, factor in factors.items():
        out[name] = (out[name] * factor).astype(out[name].dtype)
    return out
```

```python
from contextlib import ExitStack

import concourse.bass as bass
from concourse import mybir

F32 = mybir.dt.float32
BF16 = mybir.dt.bfloat16
I32 = mybir.dt.int32
ALU = mybir.AluOpType
ACT = mybir.ActivationFunctionType
AX = mybir.AxisListType

P = 128
B = 8
D = 128
H = 16
HG = 4
NG = H // HG
NEG = -1.0e30
EPS = 1e-5


def build_program(nc, x, itype, ilang, exp_wi, exp_wo, sh_wi, sh_wo, gate_vecs, gate_w1, gate_w2,
                  wq, wk, wv, wo, bo, ad_w1, ad_b1, ad_w2, ad_b2, ad_gamma, ad_beta,
                  ln1_w, c_attn, c_proj, ln2_w, router_w, moe_w1, moe_w2, out):
    NT, E, _ = gate_vecs.shape[0], exp_wi.shape[0], 0
    NS, FS = sh_wi.shape[0], sh_wi.shape[2]
    FC = FS // P
    A = ad_w1.shape[2]
    NE = router_w.shape[1]
    MC = moe_w1.shape[1] // NE // P
    DH1 = wq.shape[1] // H
    DH2 = D // H
    NCH = wq.shape[1] // P
    GB = 4
    GT = GB * P

    with ExitStack() as ctx:
        def sb(name, shape, dt=F32):
            return ctx.enter_context(nc.sbuf_tensor(name, shape, dt))

        def sem(name):
            return ctx.enter_context(nc.semaphore(name))

        bank = [ctx.enter_context(nc.psum_tensor(f"bank{i}", [P, 512], F32)) for i in range(8)]

        swi = sb("swi", [P, NS, FS])
        swo = sb("swo", [P, NS, FC, D])
        ew = [sb(f"ew{i}", [P, 4 * FS]) for i in range(3)]
        ewi = [w[:, 0:2 * FS].rearrange("p (e f) -> p e f", e=2) for w in ew]
        ewo = [w[:, 2 * FS:4 * FS].rearrange("p (e c d) -> p e c d", e=2, c=FC) for w in ew]
        gw1 = sb("gw1", [P, 4, D])
        gw2 = sb("gw2", [P, 4])
        wq_s = sb("wq_s", [P, H * DH1])
        wk_s = sb("wk_s", [P, H * DH1])
        wv_s = sb("wv_s", [P, H * DH1])
        wo_s = sb("wo_s", [P, NCH, D])
        bo_bc = sb("bo_bc", [P, D])
        aw1 = [sb(f"aw1_{i}", [P, A]) for i in range(2)]
        ab1 = [sb(f"ab1_{i}", [A, 1]) for i in range(2)]
        aw2 = [sb(f"aw2_{i}", [A, D]) for i in range(2)]
        ab2 = [sb(f"ab2_{i}", [P, D]) for i in range(2)]
        agam = [sb(f"agam{i}", [P, D]) for i in range(2)]
        abet = [sb(f"abet{i}", [P, D]) for i in range(2)]
        ln1_bc = sb("ln1_bc", [P, D])
        ln2_bc = sb("ln2_bc", [P, D])
        ca_s = sb("ca_s", [P, 3 * D])
        cp_s = sb("cp_s", [P, D])
        rw_s = sb("rw_s", [P, NE])
        hid_all = sb("hid_all", [P, 8 * 512])
        hid = [hid_all[:, i * 512:(i + 1) * 512] for i in range(8)]
        mw1 = hid_all[:, 0:NE * MC * P]
        mw2 = hid_all[:, NE * MC * P:2 * NE * MC * P].rearrange("p (c d) -> p c d", d=D)

        ident = sb("ident", [P, P])
        ident_bf = sb("ident_bf", [P, P], BF16)
        ones = sb("ones", [P, P])
        causal = sb("causal", [P, HG, P], BF16)
        headmask = sb("headmask", [P, H])
        minus_half = sb("minus_half", [P, 1])
        rank = sb("rank", [P, B, NE])

        x_all = sb("x_all", [P, B, D])
        xbo = x_all
        xT = sb("xT", [P, B, P])
        xTw = sb("xTw", [P, 2, B, P])
        eT = sb("eT", [P, B, P])
        sT = sb("sT", [P, NS, B, P])
        cT = sb("cT", [P, B, P])
        x2 = sb("x2", [P, B, D])
        idx = sb("idx", [1, 2 * B], I32)
        idx_bc = sb("idx_bc", [P, B], I32)
        idx_f = sb("idx_f", [P, B])
        gv = sb("gv", [P, NT, E])
        gvm = sb("gvm", [P, NT])
        onehot = sb("onehot", [P, NT, B])
        wpick = sb("wpick", [P, 2, NT, B])
        wab = sb("wab", [P, 2, B])
        gr = sb("gr", [P, B])
        gq = sb("gq", [P, B, 4])
        gl = sb("gl", [P, B, 4])
        gm = sb("gm", [P, B])

        q1 = [sb(f"q1_{i}", [P, NCH, P]) for i in range(2)]
        k1 = [sb(f"k1_{i}", [P, NCH, 2, P]) for i in range(2)]
        v1 = [sb(f"v1_{i}", [P, H * DH1]) for i in range(2)]
        prob = [sb(f"prob{i}", [P, H, P]) for i in range(2)]
        negmax = [sb(f"negmax{i}", [P, H]) for i in range(2)]
        rowsum = [sb(f"rowsum{i}", [P, H]) for i in range(2)]
        rinv = [sb(f"rinv{i}", [P, H]) for i in range(2)]
        probT = [sb(f"probT{i}", [P, HG, P]) for i in range(2)]
        oT1 = sb("oT1", [P, NCH, P])

        x2T = sb("x2T", [P, P])
        x2b = sb("x2b", [P, D])
        hA = sb("hA", [A, P])
        x3 = sb("x3", [P, D])
        xn = sb("xn", [P, D])
        xg = sb("xg", [P, D])
        u_all, acc, zT = sT[:, 0], sT[:, 1], sT[:, 2]
        stat = sb("stat", [P, 3, 6])
        mv = sb("mv", [P, 3, 2])
        veps = sb("veps", [P, 3])
        rstd = sb("rstd", [P, 3])
        yn = sb("yn", [P, D])
        y_s = sb("y_s", [P, D])
        yT = sb("yT", [P, P])
        qk2 = [sb(f"qk2_{i}", [P, 2, P]) for i in range(2)]
        k2 = [ew[i][:, :].rearrange("p (h k) -> p h k", h=H) for i in range(2)]
        v2 = [sb(f"v2_{i}", [P, H * (P + DH2)]) for i in range(2)]
        oT2 = sb("oT2", [P, P])
        u2 = sb("u2", [P, D])
        zn = sb("zn", [P, D])
        z_s = sb("z_s", [P, D])
        lg = sb("lg", [P, B, NE])
        r_a = sb("r_a", [P, B, NE])
        r_b = sb("r_b", [P, B, NE])
        r_c = sb("r_c", [P, B, NE])
        r_m = sb("r_m", [P, B])
        oh1 = sb("oh1", [P, B, NE])
        oh2 = sb("oh2", [P, B, NE])
        wtok = sb("wtok", [P, B, NE])
        hM = [xTw[:, i // 2, (i % 2) * GB:(i % 2 + 1) * GB, :].rearrange("p b t -> p (b t)") for i in range(4)]

        ld_idx, ld_bc, ld_x, ld_xb = sem("ld_idx"), sem("ld_bc"), sem("ld_x"), sem("ld_xb")
        ld_share = [sem(f"ld_share{i}") for i in range(NS)]
        ld_exp = [sem(f"ld_exp{i}") for i in range(3)]
        ld_gate, ld_qkv, ld_wo, ld_ffn, ld_moe = sem("ld_gate"), sem("ld_qkv"), sem("ld_wo"), sem("ld_ffn"), sem("ld_moe")
        ld_ad = [sem(f"ld_ad{i}") for i in range(2)]
        stored = sem("stored")
        id_done, const_done, pad_done, xbo_done = sem("id_done"), sem("const_done"), sem("pad_done"), sem("xbo_done")
        pool_chain, dve_chain = sem("pool_chain"), sem("dve_chain")
        xT_psum, xT_done, xTw_done = sem("xT_psum"), sem("xT_done"), sem("xTw_done")
        gv_done, gv_exp = sem("gv_done"), sem("gv_exp")
        up_done, relu_act, relu_dve, down_done = sem("up_done"), sem("relu_act"), sem("relu_dve"), sem("down_done")
        shared_out, expert_out = sem("shared_out"), sem("expert_out")
        gate_mm, gate_relu, gate_q, gate_shift, gate_exp = (sem("gate_mm"), sem("gate_relu"), sem("gate_q"),
                                                            sem("gate_shift"), sem("gate_exp"))
        combined = sem("combined")
        proj_done, qv_evac, k_evac = sem("proj_done"), sem("qv_evac"), sem("k_evac")
        scores, negmax_done, exp_done, rinv_done, norm_done = (sem("scores"), sem("negmax_done"), sem("exp_done"),
                                                               sem("rinv_done"), sem("norm_done"))
        pT_psum, pT_done, pv_done = sem("pT_psum"), sem("pT_done"), sem("pv_done")
        oT_done, wo_done, x2_done = sem("oT_done"), sem("wo_done"), sem("x2_done")
        f1_mm, x2T_done, hA_done, x2b_done = sem("f1_mm"), sem("x2T_done"), sem("hA_done"), sem("x2b_done")
        var_done, rstd_done, y_done, yT_done = sem("var_done"), sem("rstd_done"), sem("y_done"), sem("yT_done")
        u_done, qk_done, v_done, k2_done = sem("u_done"), sem("qk_done"), sem("v_done"), sem("k2_done")
        oT2_done, b_mm, u2_done, varz_done, rstdz_done = (sem("oT2_done"), sem("b_mm"), sem("u2_done"),
                                                          sem("varz_done"), sem("rstdz_done"))
        z_done, zT_done, lg_done, acc_init = sem("z_done"), sem("zT_done"), sem("lg_done"), sem("acc_init")
        r_shift, r_exp = sem("r_shift"), sem("r_exp")
        moe_up, gelu_done, moe_down, moe_acc = sem("moe_up"), sem("gelu_done"), sem("moe_down"), sem("moe_acc")

        jobs = [("shared", 0, 0), ("shared", 0, 1), ("picked", 0), ("shared", 0, 2), ("picked", 1),
                ("picked", 2), ("shared", 1, 0), ("picked", 3), ("picked", 4), ("shared", 1, 1),
                ("picked", 5), ("shared", 1, 2), ("picked", 6), ("picked", 7)]
        uses, first_use, job_of = [FC if j[0] == "shared" else 2 for j in jobs], [], []
        for k, n in enumerate(uses):
            first_use.append(len(job_of))
            job_of += [k] * n
        n_uses = len(job_of)
        picked_job = [k for k, j in enumerate(jobs) if j[0] == "picked"]

        def relu_sem(n):
            return relu_act if n % 2 == 0 else relu_dve

        block = ctx.enter_context(nc.Block())

        @block.sync
        def _(sp):
            sp.dma_start(idx[:, 0:B], itype.rearrange("(o b) -> o b", o=1)).then_inc(ld_idx, 16)
            sp.dma_start(idx[:, B:2 * B], ilang.rearrange("(o b) -> o b", o=1)).then_inc(ld_idx, 16)
            sp.dma_start(x_all[:, 0:GB, :], x[0:GB].rearrange("b t d -> t b d")).then_inc(ld_x, 16)
            sp.dma_start(swi[:, 0, :], sh_wi[0]).then_inc(ld_share[0], 16)
            sp.dma_start(x_all[:, GB:B, :], x[GB:B].rearrange("b t d -> t b d")).then_inc(ld_xb, 16)
            sp.dma_start(swo[:, 0], sh_wo[0].rearrange("(c p) d -> p c d", p=P)).then_inc(ld_share[0], 16)
            sp.wait_ge(ld_idx, 32)

            def load_experts(b):
                t = sp.value_load(idx[0:1, b:b + 1], min_val=0, max_val=E - 2)
                if b >= 3:
                    sp.wait_ge(down_done, picked_job[b - 3] + 1)
                sp.dma_start(ewi[b % 3][:, :, :], exp_wi[bass.ds(t, 2)].rearrange("e d f -> d e f")).then_inc(ld_exp[b % 3], 16)
                sp.dma_start(ewo[b % 3][:, :, :, :],
                             exp_wo[bass.ds(t, 2)].rearrange("e (c p) d -> p e c d", p=P)).then_inc(ld_exp[b % 3], 16)

            def load_adapter(b):
                n = sp.value_load(idx[0:1, B + b:B + b + 1], min_val=0, max_val=ad_w1.shape[0] - 1)
                s = b % 2
                if b >= 2:
                    sp.wait_ge(u_done, b - 1)
                row = lambda w: w[bass.ds(n, 1), :]
                sp.dma_start(aw1[s][:, :], ad_w1[bass.ds(n, 1)].rearrange("n h a -> (n h) a")).then_inc(ld_ad[s], 16)
                sp.dma_start(aw2[s][:, :], ad_w2[bass.ds(n, 1)].rearrange("n a h -> (n a) h")).then_inc(ld_ad[s], 16)
                sp.dma_start(ab1[s][:, :], row(ad_b1).rearrange("n a -> a n")).then_inc(ld_ad[s], 16)
                sp.dma_start(ab2[s][:, :], row(ad_b2).broadcast_to([P, D])).then_inc(ld_ad[s], 16)
                sp.dma_start(agam[s][:, :], row(ad_gamma).broadcast_to([P, D])).then_inc(ld_ad[s], 16)
                sp.dma_start(abet[s][:, :], row(ad_beta).broadcast_to([P, D])).then_inc(ld_ad[s], 16)

            sp.dma_start(swi[:, 1, :], sh_wi[1]).then_inc(ld_share[1], 16)
            sp.dma_start(swo[:, 1], sh_wo[1].rearrange("(c p) d -> p c d", p=P)).then_inc(ld_share[1], 16)
            load_experts(0)
            sp.dma_start(swi[:, 2, :], sh_wi[2]).then_inc(ld_share[2], 16)
            sp.dma_start(swo[:, 2], sh_wo[2].rearrange("(c p) d -> p c d", p=P)).then_inc(ld_share[2], 16)
            load_experts(1)
            load_experts(2)
            sp.dma_start(gw1[:, :, :], gate_w1.rearrange("(c p) d -> p c d", p=P)).then_inc(ld_gate, 16)
            sp.dma_start(gw2[:, :], gate_w2).then_inc(ld_gate, 16)
            sp.dma_start(wq_s[:, :], wq).then_inc(ld_qkv, 16)
            sp.dma_start(wk_s[:, :], wk).then_inc(ld_qkv, 16)
            sp.dma_start(wv_s[:, :], wv).then_inc(ld_qkv, 16)
            load_experts(3)
            sp.dma_start(wo_s[:, :, :], wo.rearrange("(c p) d -> p c d", p=P)).then_inc(ld_wo, 16)
            for b in range(4, B):
                load_experts(b)
            load_adapter(0)
            load_adapter(1)
            sp.dma_start(ln1_bc[:, :], ln1_w.rearrange("(o d) -> o d", o=1).broadcast_to([P, D])).then_inc(ld_ffn, 16)
            sp.dma_start(ln2_bc[:, :], ln2_w.rearrange("(o d) -> o d", o=1).broadcast_to([P, D])).then_inc(ld_ffn, 16)
            sp.dma_start(ca_s[:, :], c_attn).then_inc(ld_ffn, 16)
            sp.dma_start(cp_s[:, :], c_proj).then_inc(ld_ffn, 16)
            sp.dma_start(rw_s[:, :], router_w).then_inc(ld_ffn, 16)
            sp.wait_ge(down_done, len(jobs))
            sp.dma_start(mw1[:, :], moe_w1).then_inc(ld_moe, 16)
            sp.dma_start(mw2[:, :, :], moe_w2.rearrange("(c p) d -> p c d", p=P)).then_inc(ld_moe, 16)
            for b in range(2, B):
                load_adapter(b)
            for g in range(B // GB):
                sp.wait_ge(moe_acc, NE * (g + 1))
                sp.dma_start(out[g * GB:(g + 1) * GB].rearrange("b t d -> t b d"),
                             acc[:, g * GB:(g + 1) * GB, :]).then_inc(stored, 16)
            sp.wait_ge(stored, 16 * (B // GB))

        @block.gpsimd
        def _(pool):
            g = nc.gpsimd
            steps = [0]

            def link(ins):
                steps[0] += 1
                ins.then_inc(pool_chain, 1)
                pool.wait_ge(pool_chain, steps[0])

            link(g.memset(ident[:, :], 0.0))
            g.affine_select(out=ident[:, :], in_=ident[:, :], compare_op=ALU.not_equal, fill=1.0, base=0,
                            pattern=[[-1, P]], channel_multiplier=1).then_inc(id_done, 1)
            pool.wait_ge(id_done, 1)
            g.tensor_copy(ident_bf[:, :], ident[:, :]).then_inc(const_done, 1)
            g.memset(ones[:, :], 1.0).then_inc(const_done, 1)
            g.memset(minus_half[:, :], -0.5).then_inc(const_done, 1)
            link(g.memset(causal[:, :, :], 0.0))
            g.affine_select(out=causal[:, :, :], in_=causal[:, :, :], compare_op=ALU.is_ge, fill=NEG, base=0,
                            pattern=[[0, HG], [-1, P]], channel_multiplier=1).then_inc(const_done, 1)
            link(g.memset(headmask[:, :], float(DH2) ** -0.5))
            link(g.affine_select(out=headmask[:, :], in_=headmask[:, :], compare_op=ALU.is_ge, fill=0.0, base=0,
                                 pattern=[[-DH2, H]], channel_multiplier=1))
            g.affine_select(out=headmask[:, :], in_=headmask[:, :], compare_op=ALU.is_ge, fill=0.0, base=DH2 - 1,
                            pattern=[[DH2, H]], channel_multiplier=-1).then_inc(const_done, 1)
            for e in range(NE):
                g.memset(rank[:, :, e:e + 1], float(NE - e)).then_inc(const_done, 1)
            for s in range(2):
                g.memset(k1[s][:, :, :, :], 0.0).then_inc(pad_done, 1)
                g.memset(v2[s][:, :], 0.0).then_inc(pad_done, 1)
            pool.wait_ge(ld_x, 16)
            pool.wait_ge(ld_xb, 16)
            pool.wait_ge(ld_wo, 32)
            pool.wait_ge(xT_psum, B)
            g.tensor_tensor(xbo[:, :, :], x_all[:, :, :], bo_bc[:, :].unsqueeze(1).broadcast_to([P, B, D]),
                            ALU.add).then_inc(xbo_done, 1)

            def normalise(m):
                u, gr_ = divmod(m, NG)
                heads = slice(gr_ * HG, (gr_ + 1) * HG)
                pool.wait_ge(rinv_done, m + 1)
                g.tensor_tensor(prob[u % 2][:, heads, :], prob[u % 2][:, heads, :],
                                rinv[u % 2][:, heads].unsqueeze(2).broadcast_to([P, HG, P]),
                                ALU.mult).then_inc(norm_done, 1)

            for m in range(B * NG):
                normalise(m)

            def power(k, ready, count, done):
                pool.wait_ge(ready, count)
                g.tensor_tensor(rstd[:, k:k + 1], veps[:, k:k + 1], minus_half[:, :], ALU.pow).then_inc(done, 1)

            for step in range(B + 3):
                a, n, c = step, step - 1, step - 2
                if a < B:
                    pool.wait_ge(x2_done, a + 1)
                    pool.wait_ge(ld_ad[a % 2], 96 * (a // 2 + 1))
                    if a >= 1:
                        pool.wait_ge(var_done, 2 * a - 1)
                    g.tensor_tensor(x2b[:, :], x2[:, a, :], ab2[a % 2][:, :], ALU.add).then_inc(x2b_done, 1)
                for gr_ in range(NG):
                    if 0 <= n < B:
                        normalise((B + n) * NG + gr_)
                    if a < B and gr_ < 2:
                        power(gr_, var_done, 2 * a + gr_ + 1, rstd_done)
                if 0 <= c < B:
                    power(2, varz_done, c + 1, rstdz_done)
                    g.tensor_tensor(acc[:, c, :], u2[:, :], x2[:, c, :], ALU.add).then_inc(acc_init, 1)

        @block.tensor
        def _(pe):
            mm = nc.tensor.matmul

            pe.wait_ge(id_done, 1)
            for b in range(B):
                pe.wait_ge(ld_x if b < GB else ld_xb, 16)
                nc.tensor.transpose(bank[6 + b // GB][:, (b % GB) * P:(b % GB + 1) * P], x_all[:, b, :],
                                    ident[:, :]).then_inc(xT_psum, 1)

            def up(k):
                job = jobs[k]
                if job[0] == "shared":
                    _, grp, i = job
                    pe.wait_ge(ld_share[i], 32)
                    pe.wait_ge(xT_done, grp + 1)
                else:
                    b = job[1]
                    pe.wait_ge(ld_exp[b % 3], 32 * (b // 3 + 1))
                    pe.wait_ge(xTw_done, 2)
                for j in range(uses[k]):
                    n = first_use[k] + j
                    if n >= 4:
                        pe.wait_ge(relu_sem(n), (n - 4) // 2 + 1)
                    if job[0] == "shared":
                        last = mm(bank[n % 4][:, :], swi[:, i, j * P:(j + 1) * P],
                                  xT[:, grp * GB:(grp + 1) * GB, :], start=True, stop=True)
                    else:
                        for c in range(FC):
                            last = mm(bank[n % 4][:, c * P:(c + 1) * P], ewi[b % 3][:, j, c * P:(c + 1) * P],
                                      xTw[:, j, b, :], start=True, stop=True)
                    last.then_inc(up_done, 1)

            def down(k):
                job = jobs[k]
                if job[0] == "shared":
                    _, grp, i = job
                    si = grp * NS + i
                    if si >= 2:
                        pe.wait_ge(shared_out, si - 1)
                    for c in range(FC):
                        n = first_use[k] + c
                        pe.wait_ge(relu_sem(n), n // 2 + 1)
                        last = mm(bank[4 + si % 2][:, :], swo[:, i, c, :], hid[n % 8][:, :],
                                  start=(c == 0), stop=(c == FC - 1))
                else:
                    b = job[1]
                    if b >= 2:
                        pe.wait_ge(expert_out, b - 1)
                    else:
                        pe.wait_ge(xT_done, 2)
                    for j in range(2):
                        n = first_use[k] + j
                        pe.wait_ge(relu_sem(n), n // 2 + 1)
                        for c in range(FC):
                            last = mm(bank[6 + b % 2][:, 0:P], ewo[b % 3][:, j, c, :],
                                      hid[n % 8][:, c * P:(c + 1) * P],
                                      start=(j == 0 and c == 0), stop=(j == 1 and c == FC - 1))
                last.then_inc(down_done, 1)

            for k in range(len(jobs)):
                up(k)
                if k:
                    down(k - 1)
            down(len(jobs) - 1)

            pe.wait_ge(ld_gate, 32)
            pe.wait_ge(shared_out, 2 * NS)
            pe.wait_ge(expert_out, B)
            parts = [eT[:, :, 0]] + [sT[:, i, :, 0] for i in range(NS)]
            for j, part in enumerate(parts):
                last = mm(bank[0][:, 0:B], gw1[:, j, :], part, start=(j == 0), stop=(j == NS))
            last.then_inc(gate_mm, 1)
            pe.wait_ge(gate_q, 1)
            pe.wait_ge(const_done, 5 + NE)
            mm(bank[1][:, 0:B * 4], ones[:, :], gq[:, :, :], start=True, stop=True).then_inc(gate_mm, 1)

            def project(b):
                s = b % 2
                pe.wait_ge(ld_qkv, 48)
                pe.wait_ge(combined, b + 1)
                for half in range(2):
                    if b:
                        pe.wait_ge(qv_evac, 4 * b - 1 + half)
                    for c in range(4):
                        ch = 4 * half + c
                        last = mm(bank[2 + half][:, c * P:(c + 1) * P], wq_s[:, ch * P:(ch + 1) * P],
                                  cT[:, b, :], start=True, stop=True)
                    last.then_inc(proj_done, 1)
                for half in range(2):
                    pe.wait_ge(qv_evac, 4 * b + 1 + half)
                    for c in range(4):
                        ch = 4 * half + c
                        last = mm(bank[2 + half][:, c * P:(c + 1) * P], wk_s[:, ch * P:(ch + 1) * P],
                                  cT[:, b, :], start=True, stop=True)
                    last.then_inc(proj_done, 1)
                for half in range(2):
                    pe.wait_ge(k_evac, 2 * b + 1 + half)
                    mm(bank[2 + half][:, :], cT[:, b, :], wv_s[:, half * 512:(half + 1) * 512],
                       start=True, stop=True).then_inc(proj_done, 1)

            def free_scores(m):
                if m >= 2:
                    pe.wait_ge(exp_done, m - 1)

            def score1(b, g):
                m = b * NG + g
                free_scores(m)
                pe.wait_ge(qv_evac, 4 * b + 1 + g // 2)
                pe.wait_ge(k_evac, 2 * b + 1 + g // 2)
                for c in range(2):
                    ch = 2 * g + c
                    last = mm(bank[4 + m % 2][:, c * 256:(c + 1) * 256], q1[b % 2][:, ch, :],
                              k1[b % 2][:, ch, :, :], start=True, stop=True)
                last.then_inc(scores, 1)

            def transpose_probs(m):
                pe.wait_ge(norm_done, m + 1)
                if m >= 2:
                    pe.wait_ge(pT_done, m - 1)
                for h in range(HG):
                    last = nc.tensor.transpose(bank[6 + m % 2][:, h * P:(h + 1) * P],
                                               prob[m // NG % 2][:, (m % NG) * HG + h, :], ident[:, :])
                last.then_inc(pT_psum, 1)

            def values1(b, g):
                m = b * NG + g
                if g == 0 and b:
                    pe.wait_ge(x2_done, b)
                if g == 2 and b:
                    pe.wait_ge(oT_done, 2 * b)
                pe.wait_ge(qv_evac, 4 * b + 4)
                pe.wait_ge(pT_done, m + 1)
                for h in range(HG):
                    head = g * HG + h
                    ch, odd = divmod(head, 2)
                    last = mm(bank[ch // 4][odd * DH1:(odd + 1) * DH1, (ch % 4) * P:(ch % 4 + 1) * P],
                              v1[b % 2][:, head * DH1:(head + 1) * DH1], probT[m % 2][:, h, :],
                              start=True, stop=True)
                last.then_inc(pv_done, 1)

            def output1(b):
                pe.wait_ge(ld_wo, 32)
                pe.wait_ge(oT_done, 2 * b + 2)
                for c in range(NCH):
                    last = mm(bank[0][:, 0:D], oT1[:, c, :], wo_s[:, c, :], start=(c == 0), stop=(c == NCH - 1))
                last.then_inc(wo_done, 1)

            for n in range(B + 1):
                c = n - 1
                if n < B:
                    project(n)
                for g in range(NG):
                    if c >= 0:
                        transpose_probs(c * NG + g)
                    if n < B:
                        score1(n, g)
                    if c >= 0 and g >= 1:
                        values1(c, g - 1)
                if c >= 0:
                    values1(c, NG - 1)
                    output1(c)

            def adapter_transpose(a):
                pe.wait_ge(x2_done, a + 1)
                if a:
                    pe.wait_ge(v_done, a)
                nc.tensor.transpose(bank[2][:, 0:P], x2[:, a, :], ident[:, :]).then_inc(f1_mm, 1)

            def adapter_in(a):
                pe.wait_ge(ld_ad[a % 2], 96 * (a // 2 + 1))
                pe.wait_ge(x2T_done, a + 1)
                mm(bank[2][0:A, 128:256], aw1[a % 2][:, :], x2T[:, :], start=True, stop=True).then_inc(f1_mm, 1)

            def adapter_out(a):
                pe.wait_ge(hA_done, a + 1)
                mm(bank[2][:, 256:384], hA[:, :], aw2[a % 2][:, :], start=True, stop=True).then_inc(f1_mm, 1)

            def y_transpose(a):
                pe.wait_ge(y_done, a + 1)
                nc.tensor.transpose(bank[2][:, 384:512], y_s[:, :], ident[:, :]).then_inc(f1_mm, 1)

            def project2(a):
                pe.wait_ge(ld_ffn, 80)
                pe.wait_ge(yT_done, a + 1)
                mm(bank[2][:, 0:P], ca_s[:, 0:D], yT[:, :], start=True, stop=True)
                mm(bank[2][:, P:2 * P], ca_s[:, D:2 * D], yT[:, :], start=True, stop=True)
                mm(bank[2][:, 2 * P:3 * P], yT[:, :], ca_s[:, 2 * D:3 * D], start=True, stop=True).then_inc(f1_mm, 1)

            def score2(b, g):
                m = (B + b) * NG + g
                free_scores(m)
                pe.wait_ge(k2_done, b + 1)
                mm(bank[4 + m % 2][:, :], ident_bf[:, :], causal[:, :, :], start=True, stop=False)
                mm(bank[4 + m % 2][:, :], qk2[b % 2][:, 0, :], k2[b % 2][:, g * HG:(g + 1) * HG, :],
                   start=False, stop=True).then_inc(scores, 1)

            def values2(b, g):
                m = (B + b) * NG + g
                if g == 0 and b:
                    pe.wait_ge(oT2_done, b)
                pe.wait_ge(v_done, b + 1)
                pe.wait_ge(pT_done, m + 1)
                for h in range(HG):
                    head = g * HG + h
                    last = mm(bank[0][:, 0:P], v2[b % 2][:, head * P:(head + 1) * P], probT[m % 2][:, h, :],
                              start=(head == 0), stop=(head == H - 1))
                last.then_inc(pv_done, 1)

            def output2(b):
                pe.wait_ge(oT2_done, b + 1)
                if b:
                    pe.wait_ge(lg_done, b)
                mm(bank[3][:, 0:D], oT2[:, :], cp_s[:, :], start=True, stop=True).then_inc(b_mm, 1)

            def z_transpose(b):
                pe.wait_ge(z_done, b + 1)
                nc.tensor.transpose(bank[3][:, 128:256], z_s[:, :], ident[:, :]).then_inc(b_mm, 1)

            def router(b):
                pe.wait_ge(zT_done, b + 1)
                mm(bank[3][:, 256:256 + NE], zT[:, b, :], rw_s[:, :], start=True, stop=True).then_inc(b_mm, 1)

            for step in range(B + 3):
                a, n, c, r = step, step - 1, step - 2, step - 3
                has_a, has_n, has_c, has_r = (0 <= v < B for v in (a, n, c, r))
                if has_a:
                    adapter_transpose(a)
                for g in range(NG):
                    if has_c:
                        transpose_probs((B + c) * NG + g)
                    if has_n:
                        score2(n, g)
                    if has_c and g >= 1:
                        values2(c, g - 1)
                    if has_a and g == 0:
                        adapter_in(a)
                    if has_a and g == 1:
                        adapter_out(a)
                    if has_r and g == 2:
                        z_transpose(r)
                    if has_r and g == 3:
                        router(r)
                if has_c:
                    values2(c, NG - 1)
                if has_a:
                    y_transpose(a)
                if has_c:
                    output2(c)
                if has_a:
                    project2(a)

            def moe_in(k):
                g, e = divmod(k, NE)
                for c in range(MC):
                    n = MC * k + c
                    if n >= 4:
                        pe.wait_ge(gelu_done, n - 3)
                    mm(bank[n % 4][:, :], mw1[:, (e * MC + c) * P:(e * MC + c + 1) * P],
                       zT[:, g * GB:(g + 1) * GB, :], start=True, stop=True).then_inc(moe_up, 1)

            def moe_out(k):
                g, e = divmod(k, NE)
                pe.wait_ge(gelu_done, MC * (k + 1))
                if k >= 4:
                    pe.wait_ge(moe_acc, k - 3)
                for bb in range(GB):
                    for c in range(MC):
                        last = mm(bank[4 + k % 4][:, bb * P:(bb + 1) * P],
                                  hM[(MC * k + c) % 4][:, bb * P:(bb + 1) * P], mw2[:, e * MC + c, :],
                                  start=(c == 0), stop=(c == MC - 1))
                last.then_inc(moe_down, 1)

            pe.wait_ge(ld_moe, 32)
            pe.wait_ge(lg_done, B)
            pe.wait_ge(pT_done, 2 * B * NG)
            pe.wait_ge(exp_done, 2 * B * NG)
            units = 2 * NE
            for k in range(units):
                moe_in(k)
                if k:
                    moe_out(k - 1)
            moe_out(units - 1)

        @block.scalar
        def _(act):
            a_ = nc.scalar.activation
            act.dma_start(idx_bc[:, :], itype.rearrange("(o b) -> o b", o=1).broadcast_to([P, B])).then_inc(ld_bc, 16)
            act.dma_start(gv[:, :, :], gate_vecs.rearrange("(o t) e -> o t e", o=1).broadcast_to([P, NT, E])).then_inc(ld_bc, 16)
            act.dma_start(bo_bc[:, :], bo.rearrange("(o d) -> o d", o=1).broadcast_to([P, D])).then_inc(ld_wo, 16)
            act.wait_ge(gv_done, 1)
            a_(gv[:, :, :], gv[:, :, :], ACT.Exp, scale=10.0).then_inc(gv_exp, 1)

            def relu(n):
                act.wait_ge(up_done, n + 1)
                if n >= 8:
                    act.wait_ge(down_done, job_of[n - 8] + 1)
                a_(hid[n % 8][:, :], bank[n % 4][:, :], ACT.Relu).then_inc(relu_act, 1)

            def shared_evac(k):
                _, grp, i = jobs[k]
                act.wait_ge(down_done, k + 1)
                a_(sT[:, i, grp * GB:(grp + 1) * GB, :], bank[4 + (grp * NS + i) % 2][:, :],
                   ACT.Copy).then_inc(shared_out, 1)

            for k in range(len(jobs) + 1):
                if k < len(jobs):
                    for n in range(first_use[k], first_use[k] + uses[k]):
                        if n % 2 == 0:
                            relu(n)
                if k and jobs[k - 1][0] == "shared":
                    shared_evac(k - 1)
            act.wait_ge(gate_mm, 1)
            a_(gr[:, :], bank[0][:, 0:B], ACT.Relu).then_inc(gate_relu, 1)
            act.wait_ge(gate_shift, 1)
            a_(gl[:, :, :], gl[:, :, :], ACT.Exp).then_inc(gate_exp, 1)

            def exponentials(m):
                u, g = divmod(m, NG)
                act.wait_ge(negmax_done, m + 1)
                if m >= 2 * NG:
                    act.wait_ge(pT_psum, m - 2 * NG + 1)
                for h in range(HG):
                    head = g * HG + h
                    last = a_(prob[u % 2][:, head, :], bank[4 + m % 2][:, h * P:(h + 1) * P], ACT.Exp,
                              bias=negmax[u % 2][:, head:head + 1], accum_out=rowsum[u % 2][:, head:head + 1])
                last.then_inc(exp_done, 1)

            def evac_probs(m):
                act.wait_ge(pT_psum, m + 1)
                if m >= 2:
                    act.wait_ge(pv_done, m - 1)
                a_(probT[m % 2][:, :, :], bank[6 + m % 2][:, :], ACT.Copy).then_inc(pT_done, 1)

            for n in range(B + 1):
                c = n - 1
                if n < B:
                    for half in range(2):
                        act.wait_ge(proj_done, 6 * n + 1 + half)
                        if n >= 2:
                            act.wait_ge(scores, NG * (n - 1))
                        a_(q1[n % 2][:, 4 * half:4 * half + 4, :], bank[2 + half][:, :], ACT.Copy,
                           scale=float(DH1) ** -0.5).then_inc(qv_evac, 1)
                    for half in range(2):
                        act.wait_ge(proj_done, 6 * n + 5 + half)
                        if n >= 2:
                            act.wait_ge(pv_done, NG * (n - 1))
                        a_(v1[n % 2][:, half * 512:(half + 1) * 512], bank[2 + half][:, :],
                           ACT.Copy).then_inc(qv_evac, 1)
                for g in range(NG):
                    if c >= 0:
                        evac_probs(c * NG + g)
                    if n < B:
                        exponentials(n * NG + g)

            for step in range(B + 3):
                a, n, c = step, step - 1, step - 2
                for g in range(NG):
                    if 0 <= c < B:
                        evac_probs((B + c) * NG + g)
                    if 0 <= n < B:
                        exponentials((B + n) * NG + g)
                    if a < B and g == 0:
                        act.wait_ge(f1_mm, 5 * a + 2)
                        a_(hA[:, :], bank[2][0:A, 128:256], ACT.Relu, bias=ab1[a % 2][:, :]).then_inc(hA_done, 1)
                if a < B:
                    act.wait_ge(f1_mm, 5 * a + 5)
                    if a >= 2:
                        act.wait_ge(scores, NG * (B + a - 1))
                    a_(qk2[a % 2][:, :, :], bank[2][:, 0:2 * P], ACT.Copy).then_inc(qk_done, 1)

            act.wait_ge(r_shift, 1)
            a_(r_c[:, :, :], r_a[:, :, :], ACT.Exp).then_inc(r_exp, 1)
            for n in range(2 * NE * MC):
                act.wait_ge(moe_up, n + 1)
                if n >= 4:
                    act.wait_ge(moe_down, (n - 4) // MC + 1)
                a_(hM[n % 4][:, :], bank[n % 4][:, :], ACT.Gelu).then_inc(gelu_done, 1)

        @block.vector
        def _(dve):
            v = nc.vector
            steps = [0]

            def link(ins):
                steps[0] += 1
                ins.then_inc(dve_chain, 1)
                dve.wait_ge(dve_chain, steps[0])

            def bc(ap, n):
                return ap.unsqueeze(len(ap.shape)).broadcast_to(list(ap.shape) + [n])

            dve.wait_ge(ld_bc, 32)
            v.tensor_copy(idx_f[:, :], idx_bc[:, :])
            link(v.tensor_reduce(gvm[:, :], gv[:, :, :], AX.X, ALU.max))
            v.tensor_tensor(gv[:, :, :], gv[:, :, :], bc(gvm[:, :], E), ALU.subtract).then_inc(gv_done, 1)
            for half in range(2):
                dve.wait_ge(xT_psum, GB * (half + 1))
                v.tensor_copy(xT[:, half * GB:(half + 1) * GB, :], bank[6 + half][:, :]).then_inc(xT_done, 1)
            dve.wait_ge(gv_exp, 1)
            link(v.tensor_reduce(gvm[:, :], gv[:, :, :], AX.X, ALU.add))
            link(v.reciprocal(gvm[:, :], gvm[:, :]))
            link(v.tensor_tensor(gv[:, :, :], gv[:, :, :], bc(gvm[:, :], E), ALU.mult))
            for t in range(NT):
                last = v.tensor_scalar(onehot[:, t, :], idx_f[:, :], float(t), None, ALU.is_equal)
            link(last)
            for j in range(2):
                for t in range(NT):
                    last = v.tensor_scalar(wpick[:, j, t, :], onehot[:, t, :], gv[:, t, t + j:t + j + 1], None, ALU.mult)
            link(last)
            link(v.tensor_reduce(wab[:, :, :], wpick[:, :, :, :].rearrange("p j t b -> p j b t"), AX.X, ALU.add))
            dve.wait_ge(xT_done, 2)
            for j in range(2):
                v.tensor_tensor(xTw[:, j, :, :], xT[:, :, :], bc(wab[:, j, :], P), ALU.mult).then_inc(xTw_done, 1)

            def relu(n):
                dve.wait_ge(up_done, n + 1)
                if n >= 8:
                    dve.wait_ge(down_done, job_of[n - 8] + 1)
                v.tensor_scalar(hid[n % 8][:, :], bank[n % 4][:, :], 0.0, None, ALU.max).then_inc(relu_dve, 1)

            for k in range(len(jobs) + 1):
                if k < len(jobs):
                    for n in range(first_use[k], first_use[k] + uses[k]):
                        if n % 2:
                            relu(n)
                if k and jobs[k - 1][0] == "picked":
                    b = jobs[k - 1][1]
                    dve.wait_ge(down_done, k)
                    v.tensor_copy(eT[:, b, :], bank[6 + b % 2][:, 0:P]).then_inc(expert_out, 1)

            dve.wait_ge(gate_relu, 1)
            v.tensor_tensor(gq[:, :, :], bc(gr[:, :], 4), gw2[:, :].unsqueeze(1).broadcast_to([P, B, 4]),
                            ALU.mult).then_inc(gate_q, 1)
            dve.wait_ge(gate_mm, 2)
            logits = bank[1][:, 0:B * 4].rearrange("p (b j) -> p b j", j=4)
            link(v.tensor_reduce(gm[:, :], logits, AX.X, ALU.max))
            v.tensor_tensor(gl[:, :, :], logits, bc(gm[:, :], 4), ALU.subtract).then_inc(gate_shift, 1)
            dve.wait_ge(gate_exp, 1)
            link(v.tensor_reduce(gm[:, :], gl[:, :, :], AX.X, ALU.add))
            link(v.reciprocal(gm[:, :], gm[:, :]))
            link(v.tensor_tensor(gl[:, :, :], gl[:, :, :], bc(gm[:, :], 4), ALU.mult))

            def combine(b):
                if b == 0:
                    dve.wait_ge(expert_out, B)
                    dve.wait_ge(shared_out, 2 * NS)
                link(v.tensor_scalar(cT[:, b, :], eT[:, b, :], gl[:, b, 0:1], None, ALU.mult))
                for i in range(NS):
                    ins = v.scalar_tensor_tensor(cT[:, b, :], sT[:, i, b, :], gl[:, b, i + 1:i + 2], cT[:, b, :],
                                                 op0=ALU.mult, op1=ALU.add)
                    if i < NS - 1:
                        link(ins)
                ins.then_inc(combined, 1)

            def rowmax(m):
                u, g = divmod(m, NG)
                dve.wait_ge(scores, m + 1)
                v.tensor_reduce(negmax[u % 2][:, g * HG:(g + 1) * HG],
                                bank[4 + m % 2][:, :].rearrange("p (h k) -> p h k", h=HG), AX.X, ALU.max,
                                negate=True).then_inc(negmax_done, 1)

            def inverse(m):
                u, g = divmod(m, NG)
                dve.wait_ge(exp_done, m + 1)
                v.reciprocal(rinv[u % 2][:, g * HG:(g + 1) * HG],
                             rowsum[u % 2][:, g * HG:(g + 1) * HG]).then_inc(rinv_done, 1)

            def evac_k(b):
                dve.wait_ge(pad_done, 4)
                for half in range(2):
                    dve.wait_ge(proj_done, 6 * b + 3 + half)
                    if b >= 2:
                        dve.wait_ge(scores, NG * (b - 1))
                    for odd in range(2):
                        rows = slice(odd * DH1, (odd + 1) * DH1)
                        last = v.tensor_copy(k1[b % 2][rows, 4 * half:4 * half + 4, odd, :],
                                             bank[2 + half][rows, :].rearrange("p (c k) -> p c k", c=4))
                    last.then_inc(k_evac, 1)

            def evac_o(b, half):
                dve.wait_ge(pv_done, NG * b + 2 * half + 2)
                if b:
                    dve.wait_ge(wo_done, b)
                v.tensor_copy(oT1[:, 4 * half:4 * half + 4, :], bank[half][:, :]).then_inc(oT_done, 1)

            combine(0)
            for n in range(B + 1):
                c = n - 1
                if n < B:
                    evac_k(n)
                for g in range(NG):
                    if n < B:
                        rowmax(n * NG + g)
                        if g:
                            inverse(n * NG + g - 1)
                    if c >= 0 and g == 3:
                        evac_o(c, 0)
                if n < B:
                    inverse(n * NG + NG - 1)
                if c >= 0:
                    evac_o(c, 1)
                if n + 1 < B:
                    combine(n + 1)
                if c >= 0:
                    dve.wait_ge(wo_done, c + 1)
                    dve.wait_ge(xbo_done, 1)
                    v.tensor_tensor(x2[:, c, :], bank[0][:, 0:D], xbo[:, c, :], ALU.add).then_inc(x2_done, 1)

            def variance(k, src, done):
                link(v.bn_stats(stat[:, k, :], src))
                link(v.bn_aggr(mv[:, k, :], stat[:, k, :]))
                v.tensor_scalar(veps[:, k:k + 1], mv[:, k, 1:2], EPS, None, ALU.add).then_inc(done, 1)

            def standardise(k, dst, src):
                link(v.tensor_scalar(dst, src, mv[:, k, 0:1], rstd[:, k:k + 1], ALU.subtract, ALU.mult))

            dve.wait_ge(ld_ffn, 80)
            for step in range(B + 3):
                a, n, c, r = step, step - 1, step - 2, step - 3
                has_a, has_n, has_c, has_r = (0 <= w < B for w in (a, n, c, r))
                if has_a:
                    dve.wait_ge(f1_mm, 5 * a + 1)
                    v.tensor_copy(x2T[:, :], bank[2][:, 0:P]).then_inc(x2T_done, 1)
                for g in range(NG):
                    if has_n:
                        rowmax((B + n) * NG + g)
                        if g:
                            inverse((B + n) * NG + g - 1)
                    if has_a and g == 1:
                        dve.wait_ge(f1_mm, 5 * a + 3)
                        dve.wait_ge(x2b_done, a + 1)
                        link(v.tensor_tensor(x3[:, :], bank[2][:, 256:384], x2b[:, :], ALU.add))
                        variance(0, x3[:, :], var_done)
                    if has_a and g == 2:
                        dve.wait_ge(rstd_done, 2 * a + 1)
                        standardise(0, xn[:, :], x3[:, :])
                        link(v.tensor_tensor(xg[:, :], xn[:, :], agam[a % 2][:, :], ALU.mult))
                        v.tensor_tensor(u_all[:, a, :], xg[:, :], abet[a % 2][:, :], ALU.add).then_inc(u_done, 1)
                        dve.wait_ge(u_done, a + 1)
                        variance(1, u_all[:, a, :], var_done)
                    if has_r and g == 2:
                        dve.wait_ge(b_mm, 3 * r + 2)
                        v.tensor_copy(zT[:, r, :], bank[3][:, 128:256]).then_inc(zT_done, 1)
                    if has_a and g == 3:
                        dve.wait_ge(rstd_done, 2 * a + 2)
                        standardise(1, yn[:, :], u_all[:, a, :])
                        v.tensor_tensor(y_s[:, :], yn[:, :], ln1_bc[:, :], ALU.mult).then_inc(y_done, 1)
                    if has_r and g == 3:
                        dve.wait_ge(b_mm, 3 * r + 3)
                        v.tensor_copy(lg[:, r, :], bank[3][:, 256:256 + NE]).then_inc(lg_done, 1)
                if has_n:
                    inverse((B + n) * NG + NG - 1)
                if has_c:
                    dve.wait_ge(pv_done, NG * (B + c + 1))
                    v.tensor_copy(oT2[:, :], bank[0][:, 0:P]).then_inc(oT2_done, 1)
                if has_a:
                    dve.wait_ge(f1_mm, 5 * a + 4)
                    v.tensor_copy(yT[:, :], bank[2][:, 384:512]).then_inc(yT_done, 1)
                if has_c:
                    dve.wait_ge(b_mm, 3 * c + 1)
                    if c:
                        dve.wait_ge(acc_init, c)
                    link(v.tensor_tensor(u2[:, :], bank[3][:, 0:D], u_all[:, c, :], ALU.add))
                    variance(2, u2[:, :], varz_done)
                if has_a:
                    dve.wait_ge(qk_done, a + 1)
                    if a >= 2:
                        dve.wait_ge(pv_done, NG * (B + a - 1))
                    v.tensor_copy(v2[a % 2][:, :].rearrange("p (h w) -> p h w", h=H)[:, :, 0:DH2],
                                  bank[2][:, 2 * P:3 * P].rearrange("p (h d) -> p h d", h=H)).then_inc(v_done, 1)
                    dve.wait_ge(const_done, 5 + NE)
                    if a >= 2:
                        dve.wait_ge(scores, NG * (B + a - 1))
                    v.tensor_tensor(k2[a % 2][:, :, :], qk2[a % 2][:, 1:2, :].broadcast_to([P, H, P]),
                                    bc(headmask[:, :], P), ALU.mult).then_inc(k2_done, 1)
                if has_c:
                    dve.wait_ge(rstdz_done, c + 1)
                    standardise(2, zn[:, :], u2[:, :])
                    v.tensor_tensor(z_s[:, :], zn[:, :], ln2_bc[:, :], ALU.mult).then_inc(z_done, 1)

            dve.wait_ge(lg_done, B)
            link(v.tensor_reduce(r_m[:, :], lg[:, :, :], AX.X, ALU.max))
            v.tensor_tensor(r_a[:, :, :], lg[:, :, :], bc(r_m[:, :], NE), ALU.subtract).then_inc(r_shift, 1)

            def pick(dst, values):
                link(v.tensor_tensor(r_b[:, :, :], values, bc(r_m[:, :], NE), ALU.is_equal))
                link(v.tensor_tensor(r_b[:, :, :], r_b[:, :, :], rank[:, :, :], ALU.mult))
                link(v.tensor_reduce(r_m[:, :], r_b[:, :, :], AX.X, ALU.max))
                link(v.tensor_tensor(dst, rank[:, :, :], bc(r_m[:, :], NE), ALU.is_equal))

            pick(oh1[:, :, :], lg[:, :, :])
            link(v.scalar_tensor_tensor(lg[:, :, :], oh1[:, :, :], NEG, lg[:, :, :], op0=ALU.mult, op1=ALU.add))
            link(v.tensor_reduce(r_m[:, :], lg[:, :, :], AX.X, ALU.max))
            pick(oh2[:, :, :], lg[:, :, :])
            link(v.tensor_tensor(oh1[:, :, :], oh1[:, :, :], oh2[:, :, :], ALU.add))
            dve.wait_ge(r_exp, 1)
            link(v.tensor_tensor(wtok[:, :, :], r_c[:, :, :], oh1[:, :, :], ALU.mult))
            link(v.tensor_reduce(r_m[:, :], wtok[:, :, :], AX.X, ALU.add))
            link(v.reciprocal(r_m[:, :], r_m[:, :]))
            link(v.tensor_tensor(wtok[:, :, :], wtok[:, :, :], bc(r_m[:, :], NE), ALU.mult))

            dve.wait_ge(acc_init, B)
            for k in range(2 * NE):
                g, e = divmod(k, NE)
                dve.wait_ge(moe_down, k + 1)
                if e:
                    dve.wait_ge(moe_acc, k)
                for bb in range(GB):
                    b = g * GB + bb
                    last = v.scalar_tensor_tensor(acc[:, b, :], bank[4 + k % 4][:, bb * P:(bb + 1) * P],
                                                  wtok[:, b, e:e + 1], acc[:, b, :], op0=ALU.mult, op1=ALU.add)
                last.then_inc(moe_acc, 1)


_INS = ["x", "itok_B_0_2", "itok_B_0_8", "L0_cond_expert_wi", "L0_cond_expert_wo", "L0_cond_share_wi",
        "L0_cond_share_wo", "L0_cond_gate_vecs", "L0_cond_gate_w1", "L0_cond_gate_w2", "L0_attn_Wq", "L0_attn_Wk",
        "L0_attn_Wv", "L0_attn_Wo", "L0_attn_bo", "L0_cond2_W1", "L0_cond2_b1", "L0_cond2_W2", "L0_cond2_b2",
        "L0_cond2_gamma", "L0_cond2_beta", "L0_ffn_ln1_w", "L0_ffn_c_attn_w", "L0_ffn_c_proj_w", "L0_ffn_ln2_w",
        "L0_ffn_router_w", "L0_ffn_w1", "L0_ffn_w2"]
_OUT_SHAPE = (8, 128, 128)


def kernel(**inputs):
    import numpy as np
    import concourse.bacc as bacc
    from concourse.bass_utils import run_bass_kernel_spmd

    nc = bacc.Bacc("TRN2", target_bir_lowering=False, num_devices=1)
    arrays, args = {}, []
    for name in _INS:
        a = np.ascontiguousarray(inputs[name])
        arrays[f"in_{name}"] = a
        args.append(nc.dram_tensor(f"in_{name}", a.shape, mybir.dt.from_np(a.dtype), kind="ExternalInput").ap())
    args.append(nc.dram_tensor("out_0", _OUT_SHAPE, F32, kind="ExternalOutput").ap())
    build_program(nc, *args)
    result = run_bass_kernel_spmd(nc, [arrays], core_ids=[0])
    return result.results[0]["out_0"]
```

```python
from contextlib import ExitStack

import concourse.bass as bass
from concourse import mybir

F32 = mybir.dt.float32
BF16 = mybir.dt.bfloat16
I32 = mybir.dt.int32
ALU = mybir.AluOpType
ACT = mybir.ActivationFunctionType
AX = mybir.AxisListType

P = 128
B = 8
D = 128
H = 16
HG = 4
NG = H // HG
NEG = -1.0e30
EPS = 1e-5


def build_program(nc, x, itype, ilang, exp_wi, exp_wo, sh_wi, sh_wo, gate_vecs, gate_w1, gate_w2,
                  wq, wk, wv, wo, bo, ad_w1, ad_b1, ad_w2, ad_b2, ad_gamma, ad_beta,
                  ln1_w, c_attn, c_proj, ln2_w, router_w, moe_w1, moe_w2, out):
    NT, E = gate_vecs.shape[0], exp_wi.shape[0]
    NS, FS = sh_wi.shape[0], sh_wi.shape[2]
    FC = FS // P
    A = ad_w1.shape[2]
    NE = router_w.shape[1]
    MC = moe_w1.shape[1] // NE // P
    DH1 = wq.shape[1] // H
    DH2 = D // H
    NCH = wq.shape[1] // P
    GB = 4
    GT = GB * P

    with ExitStack() as ctx:
        def sb(name, shape, dt=F32):
            return ctx.enter_context(nc.sbuf_tensor(name, shape, dt))

        def sem(name):
            return ctx.enter_context(nc.semaphore(name))

        bank = [ctx.enter_context(nc.psum_tensor(f"bank{i}", [P, 512], F32)) for i in range(8)]

        sw = sb("sw", [P, 2 * NS * FS])
        swi = sw[:, 0:NS * FS].rearrange("p (e f) -> p e f", e=NS)
        swo = sw[:, NS * FS:2 * NS * FS].rearrange("p (e c d) -> p e c d", e=NS, c=FC)
        ew = [sb(f"ew{i}", [P, 4 * FS]) for i in range(3)]
        ewi = [w[:, 0:2 * FS].rearrange("p (e f) -> p e f", e=2) for w in ew]
        ewo = [w[:, 2 * FS:4 * FS].rearrange("p (e c d) -> p e c d", e=2, c=FC) for w in ew]
        gw1 = sb("gw1", [P, 4, D])
        gw2 = sb("gw2", [P, 4])
        wq_s = sb("wq_s", [P, H * DH1])
        wk_s = sb("wk_s", [P, H * DH1])
        wv_s = sb("wv_s", [P, H * DH1])
        wo_s = sb("wo_s", [P, NCH, D])
        bo_bc = sb("bo_bc", [P, D])
        aw1 = [sb(f"aw1_{i}", [P, A]) for i in range(2)]
        ab1 = [sb(f"ab1_{i}", [A, 1]) for i in range(2)]
        aw2 = [sb(f"aw2_{i}", [A, D]) for i in range(2)]
        ab2 = [sb(f"ab2_{i}", [P, D]) for i in range(2)]
        agam = [sb(f"agam{i}", [P, D]) for i in range(2)]
        abet = [sb(f"abet{i}", [P, D]) for i in range(2)]
        ln1_bc = sb("ln1_bc", [P, D])
        ln2_bc = sb("ln2_bc", [P, D])
        ca_s = sb("ca_s", [P, 3 * D])
        cp_s = sb("cp_s", [P, D])
        rw_s = sb("rw_s", [P, NE])
        hid_all = sb("hid_all", [P, 8 * 512])
        hid = [hid_all[:, i * 512:(i + 1) * 512] for i in range(8)]
        mw1 = hid_all[:, 0:NE * MC * P]
        mw2 = hid_all[:, NE * MC * P:2 * NE * MC * P].rearrange("p (c d) -> p c d", d=D)

        ident = sb("ident", [P, P])
        ident_bf = sb("ident_bf", [P, P], BF16)
        ones = sb("ones", [P, P])
        causal = sb("causal", [P, HG, P], BF16)
        headmask = sb("headmask", [P, H])
        minus_half = sb("minus_half", [P, 1])
        rank = sb("rank", [P, B, NE])

        x_all = sb("x_all", [P, B, D])
        xbo = x_all
        xT = sb("xT", [P, B, P])
        xTw = sb("xTw", [P, 2, B, P])
        eT = sb("eT", [P, B, P])
        sT = sb("sT", [P, NS, B, P])
        cT = sb("cT", [P, B, P])
        x2 = sb("x2", [P, B, D])
        idx = sb("idx", [1, 2 * B], I32)
        idx_bc = sb("idx_bc", [P, B], I32)
        idx_f = sb("idx_f", [P, B])
        gv = sb("gv", [P, NT, E])
        gvm = sb("gvm", [P, NT])
        onehot = sb("onehot", [P, NT, B])
        wpick = sb("wpick", [P, 2, NT, B])
        wab = sb("wab", [P, 2, B])
        gr = sb("gr", [P, GB])
        gq = sb("gq", [P, GB, 4])
        gl = sb("gl", [P, B, 4])
        gm = sb("gm", [P, B])

        q1 = [sb(f"q1_{i}", [P, NCH, P]) for i in range(2)]
        k1 = [sb(f"k1_{i}", [P, NCH, 2, P]) for i in range(2)]
        v1 = [sb(f"v1_{i}", [P, H * DH1]) for i in range(2)]
        prob = [[sb(f"prob{i}", [P, H, P]) for i in range(2)],
                [w[:, 0:H * P].rearrange("p (h k) -> p h k", h=H) for w in (ew[2], sw)]]
        negmax = [[sb(f"negmax{t}_{i}", [P, H]) for i in range(2)] for t in range(2)]
        rowsum = [[sb(f"rowsum{t}_{i}", [P, H]) for i in range(2)] for t in range(2)]
        rinv = [[sb(f"rinv{t}_{i}", [P, H]) for i in range(2)] for t in range(2)]
        probT = [[sb(f"probT{t}_{i}", [P, HG, P]) for i in range(2)] for t in range(2)]
        oT1 = sb("oT1", [P, NCH, P])

        x2T = sb("x2T", [P, P])
        x2b = sb("x2b", [P, D])
        hA = sb("hA", [A, P])
        x3, xn, xg, yn, y_s, u2, zn, z_s = (eT[:, i] for i in range(B))
        u_all, acc, zT = sT[:, 0], sT[:, 1], sT[:, 2]
        stat = sb("stat", [P, 3, 6])
        mv = sb("mv", [P, 3, 2])
        veps = sb("veps", [P, 3])
        rstd = sb("rstd", [P, 3])
        yT = sb("yT", [P, P])
        qk2 = [sb(f"qk2_{i}", [P, 2, P]) for i in range(2)]
        k2 = [ew[i][:, :].rearrange("p (h k) -> p h k", h=H) for i in range(2)]
        v2 = [sb(f"v2_{i}", [P, H * (P + DH2)]) for i in range(2)]
        oT2 = sb("oT2", [P, P])
        lg = sb("lg", [P, B, NE])
        r_a = sb("r_a", [P, B, NE])
        r_b = sb("r_b", [P, B, NE])
        r_c = sb("r_c", [P, B, NE])
        r_m = sb("r_m", [P, B])
        oh1 = sb("oh1", [P, B, NE])
        oh2 = sb("oh2", [P, B, NE])
        wtok = sb("wtok", [P, B, NE])
        hM = [xTw[:, i // 2, (i % 2) * GB:(i % 2 + 1) * GB, :].rearrange("p b t -> p (b t)") for i in range(4)]

        ld_idx, ld_bc, ld_x, ld_xb = sem("ld_idx"), sem("ld_bc"), sem("ld_x"), sem("ld_xb")
        ld_share = [sem(f"ld_share{i}") for i in range(NS)]
        ld_exp = [sem(f"ld_exp{i}") for i in range(3)]
        ld_gate, ld_qkv, ld_wo, ld_ffn, ld_moe = sem("ld_gate"), sem("ld_qkv"), sem("ld_wo"), sem("ld_ffn"), sem("ld_moe")
        ld_ad = [sem(f"ld_ad{i}") for i in range(2)]
        stored = sem("stored")
        id_done, const_done, pad_done, xbo_done = sem("id_done"), sem("const_done"), sem("pad_done"), sem("xbo_done")
        pool_chain, dve_chain = sem("pool_chain"), sem("dve_chain")
        xT_psum, xT_done, xTw_done = sem("xT_psum"), sem("xT_done"), sem("xTw_done")
        gv_done, gv_exp = sem("gv_done"), sem("gv_exp")
        up_done, relu_act, relu_dve, down_done = sem("up_done"), sem("relu_act"), sem("relu_dve"), sem("down_done")
        shared_out, expert_out = sem("shared_out"), sem("expert_out")
        gate_mm, gate_relu, gate_q, gate_shift, gate_exp = (sem("gate_mm"), sem("gate_relu"), sem("gate_q"),
                                                            sem("gate_shift"), sem("gate_exp"))
        combined = sem("combined")
        proj_done, qv_evac, k_evac = sem("proj_done"), sem("qv_evac"), sem("k_evac")
        scores, negmax_done, exp_done, rinv_done, norm_done, pT_psum, pT_done, pv_done = (
            [sem(f"{name}{t}") for t in (1, 2)]
            for name in ("scores", "negmax_done", "exp_done", "rinv_done", "norm_done", "pT_psum", "pT_done", "pv_done"))
        oT_done, wo_done, x2_done = sem("oT_done"), sem("wo_done"), sem("x2_done")
        f1_mm, x2T_done, hA_done, x2b_done = sem("f1_mm"), sem("x2T_done"), sem("hA_done"), sem("x2b_done")
        var_done, rstd_done, y_done, yT_done = sem("var_done"), sem("rstd_done"), sem("y_done"), sem("yT_done")
        u_done, qk_done, v_done, k2_done = sem("u_done"), sem("qk_done"), sem("v_done"), sem("k2_done")
        oT2_done, out2_psum, u2_done, varz_done, rstdz_done = (sem("oT2_done"), sem("out2_psum"), sem("u2_done"),
                                                               sem("varz_done"), sem("rstdz_done"))
        zT_psum, lg_psum = sem("zT_psum"), sem("lg_psum")
        z_done, zT_done, lg_done, acc_init = sem("z_done"), sem("zT_done"), sem("lg_done"), sem("acc_init")
        r_shift, r_exp = sem("r_shift"), sem("r_exp")
        moe_up, gelu_done, moe_down, moe_acc = sem("moe_up"), sem("gelu_done"), sem("moe_down"), sem("moe_acc")

        jobs = [("shared", 0, 0), ("shared", 0, 1), ("picked", 0), ("shared", 0, 2), ("picked", 1),
                ("picked", 2), ("picked", 3), ("shared", 1, 0), ("picked", 4), ("shared", 1, 1),
                ("picked", 5), ("shared", 1, 2), ("picked", 6), ("picked", 7)]
        uses, first_use, job_of = [FC if j[0] == "shared" else 2 for j in jobs], [], []
        for k, n in enumerate(uses):
            first_use.append(len(job_of))
            job_of += [k] * n
        n_uses = len(job_of)
        group_jobs = len(jobs) // 2
        group_uses = len(job_of) // 2
        picked_job = [k for k, j in enumerate(jobs) if j[0] == "picked"]

        b_proj, b_adapt, b_score, b_probT, b_out1, b_out2 = bank[0], bank[1], bank[2:4], bank[4:6], bank[6], bank[7]
        n_steps = B + 5
        chunks_at = {(B, "d"): (0, 1, 2, 3), (B + 1, "a"): (4,), (B + 1, "b"): (5,), (B + 1, "c"): (6,), (B + 1, "d"): (7,),
                     (B + 2, "a"): (8,), (B + 2, "b"): (9,), (B + 2, "c"): (10,), (B + 2, "d"): (11,),
                     (B + 3, 1): (12, 13), (B + 4, "a"): (14, 15)}
        units_at = {(B + 1, 0): (0,), (B + 1, 2): (1,), (B + 2, 0): (2,), (B + 2, 2): (3,), (B + 3, 0): (4,), (B + 3, 2): (5,),
                    (B + 4, "a"): (6,), (B + 4, "c"): (7,)}

        def at_step(s):
            return [e if 0 <= e < B else None for e in (s + 1, s, s - 1, s - 2, s - 3, s - 4, s - 5)]

        def hidden_bank(n):
            return bank[n % 4] if n < group_uses else (b_score[1], b_probT[1])[n % 2]

        def shared_bank(si):
            return bank[4 + si % 2] if si < NS else b_out2

        def picked_bank(b):
            return bank[6] if b < GB else b_adapt

        gate_bank = (b_score[0], b_out2)
        up_in_projection = {0: 9, 2: 10}
        down_in_projection = {1: 8, 3: 9}
        up_in_slot = {1: 11, 3: 12, 5: 13}
        down_in_slot = {0: 10, 2: 11, 4: 12, 6: 13}

        combine_in_slot = {2 * NG: 4, 2 * NG + 1: 5, 3 * NG: 6, 4 * NG: 7}

        b_moe = [b_proj, b_out1]

        def hidden_moe(n):
            return (b_score[0], b_probT[0], b_score[1], b_probT[1])[n % (2 if n < NE * MC else 4)]

        def relu_sem(n):
            return relu_act if n % 2 == 0 else relu_dve

        block = ctx.enter_context(nc.Block())

        @block.sync
        def _(sp):
            sp.dma_start(x_all[:, 0:GB, :], x[0:GB].rearrange("b t d -> t b d")).then_inc(ld_x, 16)
            sp.dma_start(swi[:, 0, :], sh_wi[0]).then_inc(ld_share[0], 16)
            sp.dma_start(x_all[:, GB:B, :], x[GB:B].rearrange("b t d -> t b d")).then_inc(ld_xb, 16)
            sp.dma_start(swo[:, 0], sh_wo[0].rearrange("(c p) d -> p c d", p=P)).then_inc(ld_share[0], 16)
            sp.dma_start(idx[:, 0:B], itype.rearrange("(o b) -> o b", o=1)).then_inc(ld_idx, 16)
            sp.dma_start(idx[:, B:2 * B], ilang.rearrange("(o b) -> o b", o=1)).then_inc(ld_idx, 16)
            sp.wait_ge(ld_idx, 32)

            def load_experts(b):
                t = sp.value_load(idx[0:1, b:b + 1], min_val=0, max_val=E - 2)
                if b >= 3:
                    sp.wait_ge(down_done, picked_job[b - 3] + 1)
                sp.dma_start(ewi[b % 3][:, :, :], exp_wi[bass.ds(t, 2)].rearrange("e d f -> d e f")).then_inc(ld_exp[b % 3], 16)
                sp.dma_start(ewo[b % 3][:, :, :, :],
                             exp_wo[bass.ds(t, 2)].rearrange("e (c p) d -> p e c d", p=P)).then_inc(ld_exp[b % 3], 16)

            def load_adapter(b):
                n = sp.value_load(idx[0:1, B + b:B + b + 1], min_val=0, max_val=ad_w1.shape[0] - 1)
                s = b % 2
                if b >= 2:
                    sp.wait_ge(u_done, b - 1)
                row = lambda w: w[bass.ds(n, 1), :]
                sp.dma_start(aw1[s][:, :], ad_w1[bass.ds(n, 1)].rearrange("n h a -> (n h) a")).then_inc(ld_ad[s], 16)
                sp.dma_start(aw2[s][:, :], ad_w2[bass.ds(n, 1)].rearrange("n a h -> (n a) h")).then_inc(ld_ad[s], 16)
                sp.dma_start(ab1[s][:, :], row(ad_b1).rearrange("n a -> a n")).then_inc(ld_ad[s], 16)
                sp.dma_start(ab2[s][:, :], row(ad_b2).broadcast_to([P, D])).then_inc(ld_ad[s], 16)
                sp.dma_start(agam[s][:, :], row(ad_gamma).broadcast_to([P, D])).then_inc(ld_ad[s], 16)
                sp.dma_start(abet[s][:, :], row(ad_beta).broadcast_to([P, D])).then_inc(ld_ad[s], 16)

            sp.dma_start(swi[:, 1, :], sh_wi[1]).then_inc(ld_share[1], 16)
            sp.dma_start(swo[:, 1], sh_wo[1].rearrange("(c p) d -> p c d", p=P)).then_inc(ld_share[1], 16)
            load_experts(0)
            sp.dma_start(swi[:, 2, :], sh_wi[2]).then_inc(ld_share[2], 16)
            sp.dma_start(swo[:, 2], sh_wo[2].rearrange("(c p) d -> p c d", p=P)).then_inc(ld_share[2], 16)
            load_experts(1)
            load_experts(2)
            sp.dma_start(gw1[:, :, :], gate_w1.rearrange("(c p) d -> p c d", p=P)).then_inc(ld_gate, 16)
            sp.dma_start(gw2[:, :], gate_w2).then_inc(ld_gate, 16)
            sp.dma_start(wq_s[:, :], wq).then_inc(ld_qkv, 16)
            sp.dma_start(wk_s[:, :], wk).then_inc(ld_qkv, 16)
            sp.dma_start(wv_s[:, :], wv).then_inc(ld_qkv, 16)
            load_experts(3)
            sp.dma_start(wo_s[:, :, :], wo.rearrange("(c p) d -> p c d", p=P)).then_inc(ld_wo, 16)
            for b in range(4, B):
                load_experts(b)
            load_adapter(0)
            load_adapter(1)
            sp.dma_start(ln1_bc[:, :], ln1_w.rearrange("(o d) -> o d", o=1).broadcast_to([P, D])).then_inc(ld_ffn, 16)
            sp.dma_start(ln2_bc[:, :], ln2_w.rearrange("(o d) -> o d", o=1).broadcast_to([P, D])).then_inc(ld_ffn, 16)
            sp.dma_start(ca_s[:, :], c_attn).then_inc(ld_ffn, 16)
            sp.dma_start(cp_s[:, :], c_proj).then_inc(ld_ffn, 16)
            sp.dma_start(rw_s[:, :], router_w).then_inc(ld_ffn, 16)
            sp.wait_ge(down_done, len(jobs))
            sp.dma_start(mw1[:, :], moe_w1).then_inc(ld_moe, 16)
            sp.dma_start(mw2[:, :, :], moe_w2.rearrange("(c p) d -> p c d", p=P)).then_inc(ld_moe, 16)
            for b in range(2, B):
                load_adapter(b)
            for g in range(B // GB):
                sp.wait_ge(moe_acc, NE * (g + 1))
                sp.dma_start(out[g * GB:(g + 1) * GB].rearrange("b t d -> t b d"),
                             acc[:, g * GB:(g + 1) * GB, :]).then_inc(stored, 16)
            sp.wait_ge(stored, 16 * (B // GB))

        @block.gpsimd
        def _(pool):
            g = nc.gpsimd
            steps = [0]

            def link(ins):
                steps[0] += 1
                ins.then_inc(pool_chain, 1)
                pool.wait_ge(pool_chain, steps[0])

            link(g.memset(ident[:, :], 0.0))
            g.affine_select(out=ident[:, :], in_=ident[:, :], compare_op=ALU.not_equal, fill=1.0, base=0,
                            pattern=[[-1, P]], channel_multiplier=1).then_inc(id_done, 1)
            pool.wait_ge(id_done, 1)
            g.tensor_copy(ident_bf[:, :], ident[:, :]).then_inc(const_done, 1)
            g.memset(ones[:, :], 1.0).then_inc(const_done, 1)
            g.memset(minus_half[:, :], -0.5).then_inc(const_done, 1)
            link(g.memset(causal[:, :, :], 0.0))
            g.affine_select(out=causal[:, :, :], in_=causal[:, :, :], compare_op=ALU.is_ge, fill=NEG, base=0,
                            pattern=[[0, HG], [-1, P]], channel_multiplier=1).then_inc(const_done, 1)
            link(g.memset(headmask[:, :], float(DH2) ** -0.5))
            link(g.affine_select(out=headmask[:, :], in_=headmask[:, :], compare_op=ALU.is_ge, fill=0.0, base=0,
                                 pattern=[[-DH2, H]], channel_multiplier=1))
            g.affine_select(out=headmask[:, :], in_=headmask[:, :], compare_op=ALU.is_ge, fill=0.0, base=DH2 - 1,
                            pattern=[[DH2, H]], channel_multiplier=-1).then_inc(const_done, 1)
            for e in range(NE):
                g.memset(rank[:, :, e:e + 1], float(NE - e)).then_inc(const_done, 1)
            for s in range(2):
                g.memset(k1[s][:, :, :, :], 0.0).then_inc(pad_done, 1)
                g.memset(v2[s][:, :], 0.0).then_inc(pad_done, 1)
            pool.wait_ge(ld_x, 16)
            pool.wait_ge(ld_xb, 16)
            pool.wait_ge(ld_wo, 32)
            pool.wait_ge(xT_psum, B)
            g.tensor_tensor(xbo[:, :, :], x_all[:, :, :], bo_bc[:, :].unsqueeze(1).broadcast_to([P, B, D]),
                            ALU.add).then_inc(xbo_done, 1)

            def normalise(t, b, gr_):
                heads = slice(gr_ * HG, (gr_ + 1) * HG)
                part = prob[t][b % 2][:, heads, :]
                pool.wait_ge(rinv_done[t], NG * b + gr_ + 1)
                g.tensor_tensor(part, part, rinv[t][b % 2][:, heads].unsqueeze(2).broadcast_to([P, HG, P]),
                                ALU.mult).then_inc(norm_done[t], 1)

            def power(k, ready, count, done):
                pool.wait_ge(ready, count)
                g.tensor_tensor(rstd[:, k:k + 1], veps[:, k:k + 1], minus_half[:, :], ALU.pow).then_inc(done, 1)

            for step in range(n_steps):
                _, n1, _, a, n2, c2, _ = at_step(step)
                if a is not None:
                    pool.wait_ge(x2_done, a + 1)
                    pool.wait_ge(ld_ad[a % 2], 96 * (a // 2 + 1))
                    if a >= 1:
                        pool.wait_ge(var_done, 2 * a - 1)
                    g.tensor_tensor(x2b[:, :], x2[:, a, :], ab2[a % 2][:, :], ALU.add).then_inc(x2b_done, 1)
                for gr_ in range(NG):
                    if n1 is not None:
                        normalise(0, n1, gr_)
                    if n2 is not None:
                        normalise(1, n2, gr_)
                    if a is not None and gr_ < 2:
                        power(gr_, var_done, 2 * a + gr_ + 1, rstd_done)
                if c2 is not None:
                    power(2, varz_done, c2 + 1, rstdz_done)
                    g.tensor_tensor(acc[:, c2, :], u2[:, :], x2[:, c2, :], ALU.add).then_inc(acc_init, 1)

        @block.tensor
        def _(pe):
            mm = nc.tensor.matmul

            pe.wait_ge(id_done, 1)
            for b in range(B):
                pe.wait_ge(ld_x if b < GB else ld_xb, 16)
                nc.tensor.transpose(bank[6 + b // GB][:, (b % GB) * P:(b % GB + 1) * P], x_all[:, b, :],
                                    ident[:, :]).then_inc(xT_psum, 1)

            def up(k):
                job = jobs[k]
                if job[0] == "shared":
                    _, grp, i = job
                    pe.wait_ge(ld_share[i], 32)
                    pe.wait_ge(xT_done, grp + 1)
                else:
                    b = job[1]
                    pe.wait_ge(ld_exp[b % 3], 32 * (b // 3 + 1))
                    pe.wait_ge(xTw_done, 2)
                for j in range(uses[k]):
                    n = first_use[k] + j
                    if n == group_uses:
                        pe.wait_ge(relu_sem(n - 1), n // 2)
                    elif n == group_uses + 1:
                        pe.wait_ge(shared_out, NS - 1)
                    elif n >= 4:
                        pe.wait_ge(relu_sem(n), (n - (4 if n < group_uses else 2)) // 2 + 1)
                    if job[0] == "shared":
                        last = mm(hidden_bank(n)[:, :], swi[:, i, j * P:(j + 1) * P],
                                  xT[:, grp * GB:(grp + 1) * GB, :], start=True, stop=True)
                    else:
                        for c in range(FC):
                            last = mm(hidden_bank(n)[:, c * P:(c + 1) * P], ewi[b % 3][:, j, c * P:(c + 1) * P],
                                      xTw[:, j, b, :], start=True, stop=True)
                    last.then_inc(up_done, 1)

            def down(k):
                job = jobs[k]
                if job[0] == "shared":
                    _, grp, i = job
                    si = grp * NS + i
                    if si >= 2:
                        pe.wait_ge(shared_out, si - 1 if si < NS else si)
                    for c in range(FC):
                        n = first_use[k] + c
                        pe.wait_ge(relu_sem(n), n // 2 + 1)
                        last = mm(shared_bank(si)[:, :], swo[:, i, c, :], hid[n % 8][:, :],
                                  start=(c == 0), stop=(c == FC - 1))
                else:
                    b = job[1]
                    if b:
                        pe.wait_ge(expert_out, b)
                    else:
                        pe.wait_ge(xT_done, 2)
                    for j in range(2):
                        n = first_use[k] + j
                        pe.wait_ge(relu_sem(n), n // 2 + 1)
                        for c in range(FC):
                            last = mm(picked_bank(b)[:, 0:P], ewo[b % 3][:, j, c, :],
                                      hid[n % 8][:, c * P:(c + 1) * P],
                                      start=(j == 0 and c == 0), stop=(j == 1 and c == FC - 1))
                last.then_inc(down_done, 1)

            def gate_in(grp):
                entries = slice(grp * GB, (grp + 1) * GB)
                pe.wait_ge(ld_gate, 32)
                pe.wait_ge(shared_out, NS * (grp + 1))
                pe.wait_ge(expert_out, GB * (grp + 1))
                pe.wait_ge(xT_done, 2)
                parts = [eT[:, entries, 0]] + [sT[:, i, entries, 0] for i in range(NS)]
                for j, part in enumerate(parts):
                    last = mm(gate_bank[grp][:, 0:GB], gw1[:, j, :], part, start=(j == 0), stop=(j == NS))
                last.then_inc(gate_mm, 1)

            def gate_out(grp):
                pe.wait_ge(gate_q, grp + 1)
                pe.wait_ge(const_done, 5 + NE)
                mm(gate_bank[grp][:, GB:GB + GB * 4], ones[:, :], gq[:, :, :], start=True, stop=True).then_inc(gate_mm, 1)

            for k in range(group_jobs):
                up(k)
                if k:
                    down(k - 1)
            down(group_jobs - 1)
            gate_in(0)
            up(group_jobs)
            gate_out(0)
            up(group_jobs + 1)
            down(group_jobs)

            def project(b, j):
                pe.wait_ge(ld_qkv, 48)
                pe.wait_ge(combined, b + 1)
                if j == 0 and b:
                    pe.wait_ge(qv_evac, 4 * b)
                elif j in (1, 2):
                    pe.wait_ge(qv_evac, 4 * b + j)
                elif j in (3, 4):
                    pe.wait_ge(k_evac, 2 * b + j - 2)
                elif j == 5:
                    pe.wait_ge(qv_evac, 4 * b + 3)
                half = j % 2
                if j < 4:
                    w = wq_s if j < 2 else wk_s
                    for c in range(4):
                        ch = 4 * half + c
                        last = mm(b_proj[:, c * P:(c + 1) * P], w[:, ch * P:(ch + 1) * P], cT[:, b, :],
                                  start=True, stop=True)
                else:
                    last = mm(b_proj[:, :], cT[:, b, :], wv_s[:, half * 512:(half + 1) * 512], start=True, stop=True)
                last.then_inc(proj_done, 1)

            def free_scores(t, m):
                if m:
                    pe.wait_ge(exp_done[t], m)

            def score1(b, g):
                free_scores(0, b * NG + g)
                pe.wait_ge(qv_evac, 4 * b + 1 + g // 2)
                pe.wait_ge(k_evac, 2 * b + 1 + g // 2)
                for c in range(2):
                    ch = 2 * g + c
                    last = mm(b_score[0][:, c * 256:(c + 1) * 256], q1[b % 2][:, ch, :],
                              k1[b % 2][:, ch, :, :], start=True, stop=True)
                last.then_inc(scores[0], 1)

            def transpose_probs(t, b, g):
                m = b * NG + g
                pe.wait_ge(norm_done[t], m + 1)
                if m:
                    pe.wait_ge(pT_done[t], m)
                for h in range(HG):
                    last = nc.tensor.transpose(b_probT[t][:, h * P:(h + 1) * P],
                                               prob[t][b % 2][:, g * HG + h, :], ident[:, :])
                last.then_inc(pT_psum[t], 1)

            def values1(b, g):
                m = b * NG + g
                if g == 0 and b:
                    pe.wait_ge(x2_done, b)
                if g == 2:
                    pe.wait_ge(oT_done, 2 * b + 1)
                pe.wait_ge(qv_evac, 4 * b + 4)
                pe.wait_ge(pT_done[0], m + 1)
                for h in range(HG):
                    head = g * HG + h
                    ch, odd = divmod(head, 2)
                    last = mm(b_out1[odd * DH1:(odd + 1) * DH1, (ch % 4) * P:(ch % 4 + 1) * P],
                              v1[b % 2][:, head * DH1:(head + 1) * DH1], probT[0][m % 2][:, h, :],
                              start=True, stop=True)
                last.then_inc(pv_done[0], 1)

            def output1(b):
                pe.wait_ge(ld_wo, 32)
                pe.wait_ge(oT_done, 2 * b + 2)
                for c in range(NCH):
                    last = mm(b_out1[:, 0:D], oT1[:, c, :], wo_s[:, c, :], start=(c == 0), stop=(c == NCH - 1))
                last.then_inc(wo_done, 1)

            def adapter_transpose(a):
                pe.wait_ge(x2_done, a + 1)
                if a:
                    pe.wait_ge(qk_done, a)
                    pe.wait_ge(v_done, a)
                nc.tensor.transpose(b_adapt[:, 0:P], x2[:, a, :], ident[:, :]).then_inc(f1_mm, 1)

            def adapter_in(a):
                pe.wait_ge(ld_ad[a % 2], 96 * (a // 2 + 1))
                pe.wait_ge(x2T_done, a + 1)
                mm(b_adapt[0:A, 128:256], aw1[a % 2][:, :], x2T[:, :], start=True, stop=True).then_inc(f1_mm, 1)

            def adapter_out(a):
                pe.wait_ge(hA_done, a + 1)
                mm(b_adapt[:, 256:384], hA[:, :], aw2[a % 2][:, :], start=True, stop=True).then_inc(f1_mm, 1)

            def y_transpose(a):
                pe.wait_ge(y_done, a + 1)
                nc.tensor.transpose(b_adapt[:, 384:512], y_s[:, :], ident[:, :]).then_inc(f1_mm, 1)

            def project2(a):
                pe.wait_ge(ld_ffn, 80)
                pe.wait_ge(yT_done, a + 1)
                mm(b_adapt[:, 0:P], ca_s[:, 0:D], yT[:, :], start=True, stop=True)
                mm(b_adapt[:, P:2 * P], ca_s[:, D:2 * D], yT[:, :], start=True, stop=True)
                mm(b_adapt[:, 2 * P:3 * P], yT[:, :], ca_s[:, 2 * D:3 * D], start=True, stop=True).then_inc(f1_mm, 1)

            def score2(b, g):
                free_scores(1, b * NG + g)
                pe.wait_ge(qk_done, b + 1)
                pe.wait_ge(k2_done, b + 1)
                mm(b_score[1][:, :], ident_bf[:, :], causal[:, :, :], start=True, stop=False)
                mm(b_score[1][:, :], qk2[b % 2][:, 0, :], k2[b % 2][:, g * HG:(g + 1) * HG, :],
                   start=False, stop=True).then_inc(scores[1], 1)

            def values2(b, g):
                m = b * NG + g
                if g == 0 and b:
                    pe.wait_ge(u2_done, b)
                pe.wait_ge(v_done, b + 1)
                pe.wait_ge(pT_done[1], m + 1)
                for h in range(HG):
                    head = g * HG + h
                    last = mm(b_out2[:, 0:P], v2[b % 2][:, head * P:(head + 1) * P], probT[1][m % 2][:, h, :],
                              start=(head == 0), stop=(head == H - 1))
                last.then_inc(pv_done[1], 1)

            def output2(b):
                pe.wait_ge(oT2_done, b + 1)
                if b:
                    pe.wait_ge(zT_done, b)
                if b and b % GB == 0:
                    pe.wait_ge(lg_done, b // GB)
                mm(b_out2[:, 128:256], oT2[:, :], cp_s[:, :], start=True, stop=True).then_inc(out2_psum, 1)

            def z_transpose(b):
                pe.wait_ge(z_done, b + 1)
                if b + 1 < B:
                    pe.wait_ge(oT2_done, b + 2)
                nc.tensor.transpose(b_out2[:, 256:384], z_s[:, :], ident[:, :]).then_inc(zT_psum, 1)

            def router(grp):
                pe.wait_ge(zT_done, GB * (grp + 1))
                for bb in range(GB):
                    last = mm(b_out2[:, 384 + bb * NE:384 + (bb + 1) * NE], zT[:, grp * GB + bb, :], rw_s[:, :],
                              start=True, stop=True)
                last.then_inc(lg_psum, 1)


            def moe_in(n):
                g, ec = divmod(n, NE * MC)
                if n == 0:
                    pe.wait_ge(ld_moe, 32)
                    pe.wait_ge(exp_done[0], B * NG)
                    pe.wait_ge(pT_done[0], B * NG)
                if n == NE * MC:
                    pe.wait_ge(exp_done[1], B * NG)
                    pe.wait_ge(pT_done[1], B * NG)
                if ec == 0:
                    pe.wait_ge(zT_done, GB * (g + 1))
                if n >= 2:
                    pe.wait_ge(gelu_done, n - (1 if n < NE * MC + 2 else 3))
                mm(hidden_moe(n)[:, :], mw1[:, ec * P:(ec + 1) * P],
                   zT[:, g * GB:(g + 1) * GB, :], start=True, stop=True).then_inc(moe_up, 1)

            def moe_out(k):
                g, e = divmod(k, NE)
                if k == 0:
                    pe.wait_ge(x2_done, B)
                pe.wait_ge(gelu_done, MC * (k + 1))
                if k >= 2:
                    pe.wait_ge(moe_acc, k - 1)
                for bb in range(GB):
                    for c in range(MC):
                        last = mm(b_moe[k % 2][:, bb * P:(bb + 1) * P],
                                  hM[(MC * k + c) % 4][:, bb * P:(bb + 1) * P], mw2[:, e * MC + c, :],
                                  start=(c == 0), stop=(c == MC - 1))
                last.then_inc(moe_down, 1)

            for j in range(6):
                project(0, j)
                if j in up_in_projection:
                    up(up_in_projection[j])
                if j in down_in_projection:
                    down(down_in_projection[j])
            def moe(step, place):
                for n in chunks_at.get((step, place), ()):
                    moe_in(n)
                for k in units_at.get((step, place), ()):
                    moe_out(k)

            for step in range(n_steps):
                pn, n1, c1, a, n2, c2, r = at_step(step)
                if step == 2:
                    gate_in(1)
                for g in range(NG):
                    slot = NG * step + g
                    if c1 is not None:
                        transpose_probs(0, c1, g)
                    if n1 is not None:
                        score1(n1, g)
                    if a is not None and g == 0:
                        adapter_transpose(a)
                    if pn is not None:
                        project(pn, g)
                    if c1 is not None and g:
                        values1(c1, g - 1)
                    if slot in up_in_slot:
                        up(up_in_slot[slot])
                    if slot in down_in_slot:
                        down(down_in_slot[slot])
                    if step == 2 and g == 0:
                        gate_out(1)
                    if c2 is not None:
                        transpose_probs(1, c2, g)
                    if n2 is not None:
                        score2(n2, g)
                    if a is not None and g == 0:
                        adapter_in(a)
                    if a is not None and g == 1:
                        adapter_out(a)
                    if c2 is not None and g:
                        values2(c2, g - 1)
                    moe(step, g)
                if c1 is not None:
                    values1(c1, NG - 1)
                if c2 is not None:
                    values2(c2, NG - 1)
                if pn is not None:
                    project(pn, 4)
                if a is not None:
                    y_transpose(a)
                if c1 is not None:
                    output1(c1)
                moe(step, "a")
                if r is not None:
                    z_transpose(r)
                if a is not None:
                    project2(a)
                if pn is not None:
                    project(pn, 5)
                moe(step, "b")
                if r is not None and r % GB == GB - 1:
                    router(r // GB)
                moe(step, "c")
                if c2 is not None:
                    output2(c2)
                moe(step, "d")
            for k in range(NE, 2 * NE):
                for c in range(MC):
                    moe_in(MC * k + c)
                if k > NE:
                    moe_out(k - 1)
            moe_out(2 * NE - 1)

        @block.scalar
        def _(act):
            a_ = nc.scalar.activation
            act.dma_start(idx_bc[:, :], itype.rearrange("(o b) -> o b", o=1).broadcast_to([P, B])).then_inc(ld_bc, 16)
            act.dma_start(gv[:, :, :], gate_vecs.rearrange("(o t) e -> o t e", o=1).broadcast_to([P, NT, E])).then_inc(ld_bc, 16)
            act.dma_start(bo_bc[:, :], bo.rearrange("(o d) -> o d", o=1).broadcast_to([P, D])).then_inc(ld_wo, 16)
            act.wait_ge(gv_done, 1)
            a_(gv[:, :, :], gv[:, :, :], ACT.Exp, scale=10.0).then_inc(gv_exp, 1)

            def relu(n):
                act.wait_ge(up_done, n + 1)
                if n >= 8:
                    act.wait_ge(down_done, job_of[n - 8] + 1)
                a_(hid[n % 8][:, :], hidden_bank(n)[:, :], ACT.Relu).then_inc(relu_act, 1)

            def shared_evac(k):
                _, grp, i = jobs[k]
                act.wait_ge(down_done, k + 1)
                a_(sT[:, i, grp * GB:(grp + 1) * GB, :], shared_bank(grp * NS + i)[:, :],
                   ACT.Copy).then_inc(shared_out, 1)

            def gate_relu_of(grp):
                act.wait_ge(gate_mm, 2 * grp + 1)
                if grp:
                    act.wait_ge(gate_q, grp)
                a_(gr[:, :], gate_bank[grp][:, 0:GB], ACT.Relu).then_inc(gate_relu, 1)

            def gate_exp_of(grp):
                part = slice(grp * GB, (grp + 1) * GB)
                act.wait_ge(gate_shift, grp + 1)
                a_(gl[:, part, :], gl[:, part, :], ACT.Exp).then_inc(gate_exp, 1)

            def relus(k):
                for n in range(first_use[k], first_use[k] + uses[k]):
                    if n % 2 == 0:
                        relu(n)

            def job_out(k):
                if jobs[k][0] == "shared":
                    shared_evac(k)

            for k in range(group_jobs):
                relus(k)
                if k:
                    job_out(k - 1)
            job_out(group_jobs - 1)
            gate_relu_of(0)
            relus(group_jobs)
            gate_exp_of(0)
            relus(group_jobs + 1)
            job_out(group_jobs)

            def exponentials(t, b, g):
                m = b * NG + g
                act.wait_ge(negmax_done[t], m + 1)
                if m >= 2 * NG:
                    act.wait_ge(pT_psum[t], m - 2 * NG + 1)
                for h in range(HG):
                    head = g * HG + h
                    last = a_(prob[t][b % 2][:, head, :], b_score[t][:, h * P:(h + 1) * P], ACT.Exp,
                              bias=negmax[t][b % 2][:, head:head + 1], accum_out=rowsum[t][b % 2][:, head:head + 1])
                last.then_inc(exp_done[t], 1)

            def evac_probs(t, b, g):
                m = b * NG + g
                act.wait_ge(pT_psum[t], m + 1)
                if m >= 2:
                    act.wait_ge(pv_done[t], m - 1)
                a_(probT[t][m % 2][:, :, :], b_probT[t][:, :], ACT.Copy).then_inc(pT_done[t], 1)

            def evac_q(b, half):
                act.wait_ge(proj_done, 6 * b + 1 + half)
                if b >= 2:
                    act.wait_ge(scores[0], NG * (b - 1))
                a_(q1[b % 2][:, 4 * half:4 * half + 4, :], b_proj[:, :], ACT.Copy,
                   scale=float(DH1) ** -0.5).then_inc(qv_evac, 1)

            def evac_v(b, half):
                act.wait_ge(proj_done, 6 * b + 5 + half)
                if b >= 2:
                    act.wait_ge(pv_done[0], NG * (b - 1))
                a_(v1[b % 2][:, half * 512:(half + 1) * 512], b_proj[:, :], ACT.Copy).then_inc(qv_evac, 1)

            def gelu(n):
                act.wait_ge(moe_up, n + 1)
                if n >= 4:
                    act.wait_ge(moe_down, (n - 4) // MC + 1)
                a_(hM[n % 4][:, :], hidden_moe(n)[:, :], ACT.Gelu).then_inc(gelu_done, 1)

            def router_exp(grp):
                part = slice(grp * GB, (grp + 1) * GB)
                act.wait_ge(r_shift, grp + 1)
                a_(r_c[:, part, :], r_a[:, part, :], ACT.Exp).then_inc(r_exp, 1)

            for j in range(6):
                if j < 2:
                    evac_q(0, j)
                elif j >= 4:
                    evac_v(0, j - 4)
                if j in up_in_projection:
                    relus(up_in_projection[j])
                if j in down_in_projection:
                    job_out(down_in_projection[j])
            for step in range(n_steps):
                pn, n1, c1, a, n2, c2, r = at_step(step)
                if step == 2:
                    gate_relu_of(1)
                for g in range(NG):
                    slot = NG * step + g
                    if c1 is not None:
                        evac_probs(0, c1, g)
                    if n1 is not None:
                        exponentials(0, n1, g)
                    if pn is not None and g < 2:
                        evac_q(pn, g)
                    if c2 is not None:
                        evac_probs(1, c2, g)
                    if slot in up_in_slot:
                        relus(up_in_slot[slot])
                    if slot in down_in_slot:
                        job_out(down_in_slot[slot])
                    if step == 2 and g == 0:
                        gate_exp_of(1)
                    if n2 is not None:
                        exponentials(1, n2, g)
                    if a is not None and g == 0:
                        act.wait_ge(f1_mm, 5 * a + 2)
                        a_(hA[:, :], b_adapt[0:A, 128:256], ACT.Relu, bias=ab1[a % 2][:, :]).then_inc(hA_done, 1)
                    for n in chunks_at.get((step, g), ()):
                        gelu(n)
                if pn is not None:
                    evac_v(pn, 0)
                    evac_v(pn, 1)
                if step == B:
                    router_exp(0)
                for place in "abcd":
                    for n in chunks_at.get((step, place), ()):
                        gelu(n)
            router_exp(1)
            for n in range(NE * MC, 2 * NE * MC):
                gelu(n)

        @block.vector
        def _(dve):
            v = nc.vector
            steps = [0]

            def link(ins):
                steps[0] += 1
                ins.then_inc(dve_chain, 1)
                dve.wait_ge(dve_chain, steps[0])

            def bc(ap, n):
                return ap.unsqueeze(len(ap.shape)).broadcast_to(list(ap.shape) + [n])

            dve.wait_ge(ld_bc, 32)
            v.tensor_copy(idx_f[:, :], idx_bc[:, :])
            link(v.tensor_reduce(gvm[:, :], gv[:, :, :], AX.X, ALU.max))
            v.tensor_tensor(gv[:, :, :], gv[:, :, :], bc(gvm[:, :], E), ALU.subtract).then_inc(gv_done, 1)
            for half in range(2):
                dve.wait_ge(xT_psum, GB * (half + 1))
                v.tensor_copy(xT[:, half * GB:(half + 1) * GB, :], bank[6 + half][:, :]).then_inc(xT_done, 1)
            dve.wait_ge(gv_exp, 1)
            link(v.tensor_reduce(gvm[:, :], gv[:, :, :], AX.X, ALU.add))
            link(v.reciprocal(gvm[:, :], gvm[:, :]))
            link(v.tensor_tensor(gv[:, :, :], gv[:, :, :], bc(gvm[:, :], E), ALU.mult))
            for t in range(NT):
                last = v.tensor_scalar(onehot[:, t, :], idx_f[:, :], float(t), None, ALU.is_equal)
            link(last)
            for j in range(2):
                for t in range(NT):
                    last = v.tensor_scalar(wpick[:, j, t, :], onehot[:, t, :], gv[:, t, t + j:t + j + 1], None, ALU.mult)
            link(last)
            link(v.tensor_reduce(wab[:, :, :], wpick[:, :, :, :].rearrange("p j t b -> p j b t"), AX.X, ALU.add))
            dve.wait_ge(xT_done, 2)
            for j in range(2):
                v.tensor_tensor(xTw[:, j, :, :], xT[:, :, :], bc(wab[:, j, :], P), ALU.mult).then_inc(xTw_done, 1)

            def relu(n):
                dve.wait_ge(up_done, n + 1)
                if n >= 8:
                    dve.wait_ge(down_done, job_of[n - 8] + 1)
                v.tensor_scalar(hid[n % 8][:, :], hidden_bank(n)[:, :], 0.0, None, ALU.max).then_inc(relu_dve, 1)

            def gate_products(grp):
                dve.wait_ge(gate_relu, grp + 1)
                if grp:
                    dve.wait_ge(gate_mm, 2 * grp)
                v.tensor_tensor(gq[:, :, :], bc(gr[:, :], 4), gw2[:, :].unsqueeze(1).broadcast_to([P, GB, 4]),
                                ALU.mult).then_inc(gate_q, 1)

            def gate_max(grp):
                part = slice(grp * GB, (grp + 1) * GB)
                dve.wait_ge(gate_mm, 2 * grp + 2)
                logits = gate_bank[grp][:, GB:GB + GB * 4].rearrange("p (b j) -> p b j", j=4)
                link(v.tensor_reduce(gm[:, part], logits, AX.X, ALU.max))
                v.tensor_tensor(gl[:, part, :], logits, bc(gm[:, part], 4), ALU.subtract).then_inc(gate_shift, 1)

            def gate_norm(grp):
                part = slice(grp * GB, (grp + 1) * GB)
                dve.wait_ge(gate_exp, grp + 1)
                link(v.tensor_reduce(gm[:, part], gl[:, part, :], AX.X, ALU.add))
                link(v.reciprocal(gm[:, part], gm[:, part]))
                link(v.tensor_tensor(gl[:, part, :], gl[:, part, :], bc(gm[:, part], 4), ALU.mult))

            def combine(b):
                grp = b // GB
                dve.wait_ge(expert_out, GB * (grp + 1))
                dve.wait_ge(shared_out, NS * (grp + 1))
                link(v.tensor_scalar(cT[:, b, :], eT[:, b, :], gl[:, b, 0:1], None, ALU.mult))
                for i in range(NS):
                    ins = v.scalar_tensor_tensor(cT[:, b, :], sT[:, i, b, :], gl[:, b, i + 1:i + 2], cT[:, b, :],
                                                 op0=ALU.mult, op1=ALU.add)
                    if i < NS - 1:
                        link(ins)
                ins.then_inc(combined, 1)

            def relus(k):
                for n in range(first_use[k], first_use[k] + uses[k]):
                    if n % 2:
                        relu(n)

            def job_out(k):
                if jobs[k][0] == "picked":
                    b = jobs[k][1]
                    dve.wait_ge(down_done, k + 1)
                    v.tensor_copy(eT[:, b, :], picked_bank(b)[:, 0:P]).then_inc(expert_out, 1)

            for k in range(group_jobs):
                relus(k)
                if k:
                    job_out(k - 1)
            job_out(group_jobs - 1)
            gate_products(0)
            relus(group_jobs)
            gate_max(0)
            relus(group_jobs + 1)
            job_out(group_jobs)
            gate_norm(0)
            combine(0)
            combine(1)

            def rowmax(t, b, g):
                dve.wait_ge(scores[t], NG * b + g + 1)
                v.tensor_reduce(negmax[t][b % 2][:, g * HG:(g + 1) * HG],
                                b_score[t][:, :].rearrange("p (h k) -> p h k", h=HG), AX.X, ALU.max,
                                negate=True).then_inc(negmax_done[t], 1)

            def inverse(t, b, g):
                dve.wait_ge(exp_done[t], NG * b + g + 1)
                v.reciprocal(rinv[t][b % 2][:, g * HG:(g + 1) * HG],
                             rowsum[t][b % 2][:, g * HG:(g + 1) * HG]).then_inc(rinv_done[t], 1)

            def evac_k(b, half):
                dve.wait_ge(pad_done, 4)
                dve.wait_ge(proj_done, 6 * b + 3 + half)
                if b >= 2:
                    dve.wait_ge(scores[0], NG * (b - 1))
                for odd in range(2):
                    rows = slice(odd * DH1, (odd + 1) * DH1)
                    last = v.tensor_copy(k1[b % 2][rows, 4 * half:4 * half + 4, odd, :],
                                         b_proj[rows, :].rearrange("p (c k) -> p c k", c=4))
                last.then_inc(k_evac, 1)

            def evac_o(b, half):
                dve.wait_ge(pv_done[0], NG * b + 2 * half + 2)
                if b:
                    dve.wait_ge(wo_done, b)
                v.tensor_copy(oT1[:, 4 * half:4 * half + 4, :], b_out1[:, :]).then_inc(oT_done, 1)

            def variance(k, src, done):
                link(v.bn_stats(stat[:, k, :], src))
                link(v.bn_aggr(mv[:, k, :], stat[:, k, :]))
                v.tensor_scalar(veps[:, k:k + 1], mv[:, k, 1:2], EPS, None, ALU.add).then_inc(done, 1)

            def standardise(k, dst, src):
                link(v.tensor_scalar(dst, src, mv[:, k, 0:1], rstd[:, k:k + 1], ALU.subtract, ALU.mult))

            def router_shift(grp):
                part = slice(grp * GB, (grp + 1) * GB)
                dve.wait_ge(lg_psum, grp + 1)
                v.tensor_copy(lg[:, part, :], b_out2[:, 384:384 + GB * NE]).then_inc(lg_done, 1)
                dve.wait_ge(lg_done, grp + 1)
                link(v.tensor_reduce(r_m[:, part], lg[:, part, :], AX.X, ALU.max))
                v.tensor_tensor(r_a[:, part, :], lg[:, part, :], bc(r_m[:, part], NE), ALU.subtract).then_inc(r_shift, 1)

            def router_weights(grp):
                part = slice(grp * GB, (grp + 1) * GB)
                lg_, b_, rk = lg[:, part, :], r_b[:, part, :], rank[:, part, :]
                o1, o2, w_, m_ = oh1[:, part, :], oh2[:, part, :], wtok[:, part, :], r_m[:, part]

                def pick(dst):
                    link(v.tensor_tensor(b_, lg_, bc(m_, NE), ALU.is_equal))
                    link(v.tensor_tensor(b_, b_, rk, ALU.mult))
                    link(v.tensor_reduce(m_, b_, AX.X, ALU.max))
                    link(v.tensor_tensor(dst, rk, bc(m_, NE), ALU.is_equal))

                pick(o1)
                link(v.scalar_tensor_tensor(lg_, o1, NEG, lg_, op0=ALU.mult, op1=ALU.add))
                link(v.tensor_reduce(m_, lg_, AX.X, ALU.max))
                pick(o2)
                link(v.tensor_tensor(o1, o1, o2, ALU.add))
                dve.wait_ge(r_exp, grp + 1)
                link(v.tensor_tensor(w_, r_c[:, part, :], o1, ALU.mult))
                link(v.tensor_reduce(m_, w_, AX.X, ALU.add))
                link(v.reciprocal(m_, m_))
                link(v.tensor_tensor(w_, w_, bc(m_, NE), ALU.mult))

            def moe_add(k):
                g, e = divmod(k, NE)
                if e == 0:
                    dve.wait_ge(acc_init, GB * (g + 1))
                dve.wait_ge(moe_down, k + 1)
                if e:
                    dve.wait_ge(moe_acc, k)
                for bb in range(GB):
                    b = g * GB + bb
                    last = v.scalar_tensor_tensor(acc[:, b, :], (b_proj, b_out1)[k % 2][:, bb * P:(bb + 1) * P],
                                                  wtok[:, b, e:e + 1], acc[:, b, :], op0=ALU.mult, op1=ALU.add)
                last.then_inc(moe_acc, 1)

            for j in range(6):
                if j in (2, 3):
                    evac_k(0, j - 2)
                if j in up_in_projection:
                    relus(up_in_projection[j])
                if j in down_in_projection:
                    job_out(down_in_projection[j])
            for b in range(2, GB):
                combine(b)
            for step in range(n_steps):
                pn, n1, c1, a, n2, c2, r = at_step(step)
                if step == 2:
                    gate_products(1)
                for g in range(NG):
                    slot = NG * step + g
                    if n1 is not None:
                        rowmax(0, n1, g)
                        if g:
                            inverse(0, n1, g - 1)
                    if a is not None and g == 0:
                        dve.wait_ge(f1_mm, 5 * a + 1)
                        v.tensor_copy(x2T[:, :], b_adapt[:, 0:P]).then_inc(x2T_done, 1)
                    if pn is not None and g >= 2:
                        evac_k(pn, g - 2)
                    if a is not None and g == 2:
                        dve.wait_ge(rstd_done, 2 * a + 1)
                        standardise(0, xn[:, :], x3[:, :])
                        link(v.tensor_tensor(xg[:, :], xn[:, :], agam[a % 2][:, :], ALU.mult))
                        v.tensor_tensor(u_all[:, a, :], xg[:, :], abet[a % 2][:, :], ALU.add).then_inc(u_done, 1)
                        dve.wait_ge(u_done, a + 1)
                        variance(1, u_all[:, a, :], var_done)
                    if slot in up_in_slot:
                        relus(up_in_slot[slot])
                    if slot in down_in_slot:
                        job_out(down_in_slot[slot])
                    if step == 2 and g == 0:
                        gate_max(1)
                        gate_norm(1)
                    if n2 is not None:
                        rowmax(1, n2, g)
                        if g:
                            inverse(1, n2, g - 1)
                    if slot in combine_in_slot:
                        combine(combine_in_slot[slot])
                    if c1 is not None and g == 2:
                        evac_o(c1, 0)
                    if a is not None and g == 1:
                        dve.wait_ge(f1_mm, 5 * a + 3)
                        dve.wait_ge(x2b_done, a + 1)
                        link(v.tensor_tensor(x3[:, :], b_adapt[:, 256:384], x2b[:, :], ALU.add))
                        variance(0, x3[:, :], var_done)
                    if a is not None and g == 3:
                        dve.wait_ge(rstd_done, 2 * a + 2)
                        standardise(1, yn[:, :], u_all[:, a, :])
                        dve.wait_ge(ld_ffn, 80)
                        v.tensor_tensor(y_s[:, :], yn[:, :], ln1_bc[:, :], ALU.mult).then_inc(y_done, 1)
                    if r is not None and g == 1:
                        dve.wait_ge(rstdz_done, r + 1)
                        standardise(2, zn[:, :], u2[:, :])
                        v.tensor_tensor(z_s[:, :], zn[:, :], ln2_bc[:, :], ALU.mult).then_inc(z_done, 1)
                    for k in units_at.get((step, g), ()):
                        moe_add(k)
                if n1 is not None:
                    inverse(0, n1, NG - 1)
                if c1 is not None:
                    evac_o(c1, 1)
                if n2 is not None:
                    inverse(1, n2, NG - 1)
                if c2 is not None:
                    dve.wait_ge(pv_done[1], NG * (c2 + 1))
                    v.tensor_copy(oT2[:, :], b_out2[:, 0:P]).then_inc(oT2_done, 1)
                if a is not None:
                    dve.wait_ge(f1_mm, 5 * a + 4)
                    v.tensor_copy(yT[:, :], b_adapt[:, 384:512]).then_inc(yT_done, 1)
                if c1 is not None:
                    dve.wait_ge(wo_done, c1 + 1)
                    dve.wait_ge(xbo_done, 1)
                    v.tensor_tensor(x2[:, c1, :], b_out1[:, 0:D], xbo[:, c1, :], ALU.add).then_inc(x2_done, 1)
                if r is not None:
                    dve.wait_ge(zT_psum, r + 1)
                    v.tensor_copy(zT[:, r, :], b_out2[:, 256:384]).then_inc(zT_done, 1)
                if a is not None:
                    dve.wait_ge(f1_mm, 5 * a + 5)
                    if a >= 2:
                        dve.wait_ge(scores[1], NG * (a - 1))
                    v.tensor_copy(qk2[a % 2][:, :, :], b_adapt[:, 0:2 * P]).then_inc(qk_done, 1)
                    if a >= 2:
                        dve.wait_ge(pv_done[1], NG * (a - 1))
                    v.tensor_copy(v2[a % 2][:, :].rearrange("p (h w) -> p h w", h=H)[:, :, 0:DH2],
                                  b_adapt[:, 2 * P:3 * P].rearrange("p (h d) -> p h d", h=H)).then_inc(v_done, 1)
                if r is not None and r % GB == GB - 1:
                    router_shift(r // GB)
                if a is not None:
                    dve.wait_ge(const_done, 5 + NE)
                    dve.wait_ge(qk_done, a + 1)
                    v.tensor_tensor(k2[a % 2][:, :, :], qk2[a % 2][:, 1:2, :].broadcast_to([P, H, P]),
                                    bc(headmask[:, :], P), ALU.mult).then_inc(k2_done, 1)
                if c2 is not None:
                    dve.wait_ge(out2_psum, c2 + 1)
                    if c2:
                        dve.wait_ge(acc_init, c2)
                    v.tensor_tensor(u2[:, :], b_out2[:, 128:256], u_all[:, c2, :], ALU.add).then_inc(u2_done, 1)
                    dve.wait_ge(u2_done, c2 + 1)
                    variance(2, u2[:, :], varz_done)
                for place in "abcd":
                    for k in units_at.get((step, place), ()):
                        moe_add(k)
                if r is not None and r % GB == GB - 1:
                    router_weights(r // GB)
            for k in range(NE, 2 * NE):
                moe_add(k)


_INS = ["x", "itok_B_0_2", "itok_B_0_8", "L0_cond_expert_wi", "L0_cond_expert_wo", "L0_cond_share_wi",
        "L0_cond_share_wo", "L0_cond_gate_vecs", "L0_cond_gate_w1", "L0_cond_gate_w2", "L0_attn_Wq", "L0_attn_Wk",
        "L0_attn_Wv", "L0_attn_Wo", "L0_attn_bo", "L0_cond2_W1", "L0_cond2_b1", "L0_cond2_W2", "L0_cond2_b2",
        "L0_cond2_gamma", "L0_cond2_beta", "L0_ffn_ln1_w", "L0_ffn_c_attn_w", "L0_ffn_c_proj_w", "L0_ffn_ln2_w",
        "L0_ffn_router_w", "L0_ffn_w1", "L0_ffn_w2"]
_OUT_SHAPE = (8, 128, 128)


def kernel(**inputs):
    import numpy as np
    import concourse.bacc as bacc
    from concourse.bass_utils import run_bass_kernel_spmd

    nc = bacc.Bacc("TRN2", target_bir_lowering=False, num_devices=1)
    arrays, args = {}, []
    for name in _INS:
        a = np.ascontiguousarray(inputs[name])
        arrays[f"in_{name}"] = a
        args.append(nc.dram_tensor(f"in_{name}", a.shape, mybir.dt.from_np(a.dtype), kind="ExternalInput").ap())
    args.append(nc.dram_tensor("out_0", _OUT_SHAPE, F32, kind="ExternalOutput").ap())
    build_program(nc, *args)
    result = run_bass_kernel_spmd(nc, [arrays], core_ids=[0])
    return result.results[0]["out_0"]
```
